# Optimizing a Trainium2 kernel written in Bass

```python
import numpy as np
import jax
import jax.numpy as jnp

def _softmax(x, axis=-1):
    return jax.nn.softmax(x, axis=axis)

def _gelu(x):
    return jax.nn.gelu(x, approximate=True)

def _silu(x):
    return jax.nn.silu(x)

def _sigmoid(x):
    return jax.nn.sigmoid(x)

def _layernorm(x, axis=-1, eps=1e-05):
    m = jnp.mean(x, axis=axis, keepdims=True)
    v = jnp.var(x, axis=axis, keepdims=True)
    return (x - m) / jnp.sqrt(v + eps)

def _scatter_add(tgt, idx, src, axis=0):
    return tgt.at[idx].add(src)

def _segment_sum(src, seg, n):
    return jax.ops.segment_sum(src, seg, n)
kernel_name = 'mk_seq_postln_d2_jaxref_r8_1ddf5a'

def setup_inputs(seed: int=0):
    np.random.seed(seed)
    _w = jnp.asarray

    def _L0_attn_setup():
        import jax, jax.numpy as jnp
        import numpy as np
        B, N, D = (8, 128, 512)
        H = 8
        HEAD_DIM = D // H
        E = HEAD_DIM // H
        key = jax.random.key(seed)
        ks = jax.random.split(key, 7)
        s = 0.02
        return {'x': jax.random.normal(ks[0], (B, N, D), dtype=jnp.float32), 'Wqk_w': jax.random.normal(ks[1], (2 * HEAD_DIM, D), dtype=jnp.float32) * s, 'Wqk_b': jnp.zeros((2 * HEAD_DIM,), dtype=jnp.float32), 'Wv_w': jax.random.normal(ks[2], (HEAD_DIM, D), dtype=jnp.float32) * s, 'Wv_b': jnp.zeros((HEAD_DIM,), dtype=jnp.float32), 'Wo_w': jax.random.normal(ks[3], (D, HEAD_DIM), dtype=jnp.float32) * s, 'Wo_b': jnp.zeros((D,), dtype=jnp.float32)}
    _L0_attn_in = _L0_attn_setup()

    def _L0_ffn_setup():
        import jax, jax.numpy as jnp
        import numpy as np
        BS = 128
        FP8_MAX = 448.0

        def act_quant(x):
            T, K = x.shape
            xb = x.reshape(T, K // BS, BS)
            amax = jnp.max(jnp.abs(xb), axis=-1)
            scale = amax / FP8_MAX + 1e-12
            xq = (xb / scale[:, :, None]).reshape(T, K)
            return (xq, scale)

        def linear_dsv3(x, wq, w_scale):
            T, K = x.shape
            N = wq.shape[0]
            xq, xs = act_quant(x)
            xdq = (xq.reshape(T, K // BS, BS) * xs[:, :, None]).reshape(T, K)
            wdq = (wq.reshape(N // BS, BS, K // BS, BS) * w_scale[:, None, :, None]).reshape(N, K)
            return xdq @ wdq.T
        key = jax.random.key(seed)
        ks = jax.random.split(key, 4)
        DIM, INTER = (512, 1792)

        def make_qweight(k, n, m):
            w = jax.random.normal(k, (n, m), dtype=jnp.float32) * 0.02
            wb = w.reshape(n // BS, BS, m // BS, BS)
            amax = jnp.max(jnp.abs(wb), axis=(1, 3))
            scale = amax / FP8_MAX + 1e-12
            wq = (wb / scale[:, None, :, None]).reshape(n, m)
            return (wq, scale)
        x = jax.random.normal(ks[0], (2, 128, DIM), dtype=jnp.float32)
        w1, w1_scale = make_qweight(ks[1], INTER, DIM)
        w3, w3_scale = make_qweight(ks[2], INTER, DIM)
        w2, w2_scale = make_qweight(ks[3], DIM, INTER)
        return {'x': x, 'w1': w1, 'w1_scale': w1_scale, 'w3': w3, 'w3_scale': w3_scale, 'w2': w2, 'w2_scale': w2_scale}
    _L0_ffn_in = _L0_ffn_setup()

    def _L1_attn_setup():
        import jax, jax.numpy as jnp
        import numpy as np
        HIDDEN = 512
        NUM_HEADS = 32
        HEAD_DIM = HIDDEN // NUM_HEADS

        def _fp8_roundtrip(x):
            return x.astype(jnp.float8_e4m3fn).astype(jnp.float32)
        key = jax.random.key(seed)
        ks = jax.random.split(key, 10)
        B, S = (2, 512)
        hidden_states = jax.random.normal(ks[0], (B, S, HIDDEN), dtype=jnp.float32)
        scale = 0.02

        def lin(kw, kb):
            w = jax.random.normal(kw, (HIDDEN, HIDDEN), dtype=jnp.float32) * scale
            b = jax.random.normal(kb, (HIDDEN,), dtype=jnp.float32) * scale
            return (w, b)
        wq, bq = lin(ks[1], ks[2])
        wk, bk = lin(ks[3], ks[4])
        wv, bv = lin(ks[5], ks[6])
        wl, bl = lin(ks[7], ks[8])
        wq, bq = (_fp8_roundtrip(wq), _fp8_roundtrip(bq))
        wk, bk = (_fp8_roundtrip(wk), _fp8_roundtrip(bk))
        wv, bv = (_fp8_roundtrip(wv), _fp8_roundtrip(bv))
        return {'hidden_states': hidden_states, 'wq': wq, 'bq': bq, 'wk': wk, 'bk': bk, 'wv': wv, 'bv': bv, 'wl': wl, 'bl': bl}
    _L1_attn_in = _L1_attn_setup()

    def _L1_ffn_setup():
        import jax, jax.numpy as jnp
        import numpy as np
        HIDDEN = 512
        INTER = 1376
        BATCH, SEQ = (2, 256)

        def _ternary(key, shape):
            return jax.random.randint(key, shape, -1, 2).astype(jnp.float32)
        key = jax.random.key(seed)
        kx, kg, ku, kd = jax.random.split(key, 4)
        x = jax.random.normal(kx, (BATCH, SEQ, HIDDEN), dtype=jnp.float32)
        gate_w = _ternary(kg, (INTER, HIDDEN))
        up_w = _ternary(ku, (INTER, HIDDEN))
        down_w = _ternary(kd, (HIDDEN, INTER))
        gate_scale = jnp.float32(0.02)
        up_scale = jnp.float32(0.02)
        down_scale = jnp.float32(0.02)
        return {'x': x, 'gate_w': gate_w, 'up_w': up_w, 'down_w': down_w, 'gate_scale': gate_scale, 'up_scale': up_scale, 'down_scale': down_scale}
    _L1_ffn_in = _L1_ffn_setup()
    _d = {'L0_attn_x': _L0_attn_in['x'], 'L0_attn_Wqk_w': _L0_attn_in['Wqk_w'], 'L0_attn_Wqk_b': _L0_attn_in['Wqk_b'], 'L0_attn_Wv_w': _L0_attn_in['Wv_w'], 'L0_attn_Wv_b': _L0_attn_in['Wv_b'], 'L0_attn_Wo_w': _L0_attn_in['Wo_w'], 'L0_attn_Wo_b': _L0_attn_in['Wo_b'], 'L0_ffn_w1': _L0_ffn_in['w1'], 'L0_ffn_w1_scale': _L0_ffn_in['w1_scale'], 'L0_ffn_w3': _L0_ffn_in['w3'], 'L0_ffn_w3_scale': _L0_ffn_in['w3_scale'], 'L0_ffn_w2': _L0_ffn_in['w2'], 'L0_ffn_w2_scale': _L0_ffn_in['w2_scale'], 'L1_attn_wq': _L1_attn_in['wq'], 'L1_attn_bq': _L1_attn_in['bq'], 'L1_attn_wk': _L1_attn_in['wk'], 'L1_attn_bk': _L1_attn_in['bk'], 'L1_attn_wv': _L1_attn_in['wv'], 'L1_attn_bv': _L1_attn_in['bv'], 'L1_attn_wl': _L1_attn_in['wl'], 'L1_attn_bl': _L1_attn_in['bl'], 'L1_ffn_gate_w': _L1_ffn_in['gate_w'], 'L1_ffn_up_w': _L1_ffn_in['up_w'], 'L1_ffn_down_w': _L1_ffn_in['down_w'], 'L1_ffn_gate_scale': _L1_ffn_in['gate_scale'], 'L1_ffn_up_scale': _L1_ffn_in['up_scale'], 'L1_ffn_down_scale': _L1_ffn_in['down_scale']}
    _x0 = _d['L0_attn_x']
    _d['L0_attn_x'] = jax.random.normal(jax.random.fold_in(jax.random.key(seed), 1), (2, 512, 512), dtype=_x0.dtype)
    del _x0
    return _d

def reference(L0_attn_x, L0_attn_Wqk_w, L0_attn_Wqk_b, L0_attn_Wv_w, L0_attn_Wv_b, L0_attn_Wo_w, L0_attn_Wo_b, L0_ffn_w1, L0_ffn_w1_scale, L0_ffn_w3, L0_ffn_w3_scale, L0_ffn_w2, L0_ffn_w2_scale, L1_attn_wq, L1_attn_bq, L1_attn_wk, L1_attn_bk, L1_attn_wv, L1_attn_bv, L1_attn_wl, L1_attn_bl, L1_ffn_gate_w, L1_ffn_up_w, L1_ffn_down_w, L1_ffn_gate_scale, L1_ffn_up_scale, L1_ffn_down_scale):

    def _L0_attn_ref(x, Wqk_w, Wqk_b, Wv_w, Wv_b, Wo_w, Wo_b):
        import jax, jax.numpy as jnp
        import numpy as np
        B, N, D = (8, 128, 512)
        H = 8
        HEAD_DIM = D // H
        E = HEAD_DIM // H
        b, n, _ = x.shape
        qk = (x @ Wqk_w.T + Wqk_b).reshape(b, n, H, E, 2)
        q = jnp.transpose(qk[..., 0], (0, 2, 1, 3))
        k = jnp.transpose(qk[..., 1], (0, 2, 1, 3))
        v = (x @ Wv_w.T + Wv_b).reshape(b, n, H, E)
        v = jnp.transpose(v, (0, 2, 1, 3))
        scores = jnp.einsum('bhqd,bhkd->bhqk', q, k)
        attn = jax.nn.softmax(scores, axis=-1) / jnp.asarray(HEAD_DIM ** 0.5, x.dtype)
        out = jnp.einsum('bhsl,bhlv->bhsv', attn, v)
        out = jnp.transpose(out, (0, 2, 1, 3)).reshape(b, n, H * E)
        return out @ Wo_w.T + Wo_b

    def _L0_ffn_ref(x, w1, w1_scale, w3, w3_scale, w2, w2_scale):
        import jax, jax.numpy as jnp
        import numpy as np
        BS = 128
        FP8_MAX = 448.0

        def act_quant(x):
            T, K = x.shape
            xb = x.reshape(T, K // BS, BS)
            amax = jnp.max(jnp.abs(xb), axis=-1)
            scale = amax / FP8_MAX + 1e-12
            xq = (xb / scale[:, :, None]).reshape(T, K)
            return (xq, scale)

        def linear_dsv3(x, wq, w_scale):
            T, K = x.shape
            N = wq.shape[0]
            xq, xs = act_quant(x)
            xdq = (xq.reshape(T, K // BS, BS) * xs[:, :, None]).reshape(T, K)
            wdq = (wq.reshape(N // BS, BS, K // BS, BS) * w_scale[:, None, :, None]).reshape(N, K)
            return xdq @ wdq.T
        B, S, D = x.shape
        xf = x.reshape(-1, D)
        g = linear_dsv3(xf, w1, w1_scale)
        u = linear_dsv3(xf, w3, w3_scale)
        h = jax.nn.silu(g) * u
        y = linear_dsv3(h, w2, w2_scale)
        return y.reshape(B, S, D)

    def _L1_attn_ref(hidden_states, wq, bq, wk, bk, wv, bv, wl, bl):
        import jax, jax.numpy as jnp
        import numpy as np
        HIDDEN = 512
        NUM_HEADS = 32
        HEAD_DIM = HIDDEN // NUM_HEADS

        def _fp8_roundtrip(x):
            return x.astype(jnp.float8_e4m3fn).astype(jnp.float32)
        B, S, E = hidden_states.shape
        H, D = (NUM_HEADS, HEAD_DIM)
        q = (hidden_states @ wq.T + bq).reshape(B, S, H, D)
        k = (hidden_states @ wk.T + bk).reshape(B, S, H, D)
        v = (hidden_states @ wv.T + bv).reshape(B, S, H, D)
        latent = hidden_states @ wl.T + bl
        scores = jnp.einsum('bshd,bstd->bsht', q, k) / np.sqrt(D).astype(np.float32)
        probs = jax.nn.softmax(scores, axis=-1)
        context = jnp.einsum('bsht,bstd->bshd', probs, v).reshape(B, S, E)
        return context

    def _L1_ffn_ref(x, gate_w, up_w, down_w, gate_scale, up_scale, down_scale):
        import jax, jax.numpy as jnp
        import numpy as np
        HIDDEN = 512
        INTER = 1376
        BATCH, SEQ = (2, 256)

        def _ternary(key, shape):
            return jax.random.randint(key, shape, -1, 2).astype(jnp.float32)
        gate = jnp.einsum('bsh,ih->bsi', x, gate_w) * gate_scale
        up = jnp.einsum('bsh,ih->bsi', x, up_w) * up_scale
        inter = jax.nn.silu(gate) * up
        out = jnp.einsum('bsi,hi->bsh', inter, down_w) * down_scale
        return out
    x = L0_attn_x
    x = _layernorm(x + _L0_attn_ref(x, L0_attn_Wqk_w, L0_attn_Wqk_b, L0_attn_Wv_w, L0_attn_Wv_b, L0_attn_Wo_w, L0_attn_Wo_b), axis=-1)
    x = _layernorm(x + _L0_ffn_ref(x, L0_ffn_w1, L0_ffn_w1_scale, L0_ffn_w3, L0_ffn_w3_scale, L0_ffn_w2, L0_ffn_w2_scale), axis=-1)
    x = _layernorm(x + _L1_attn_ref(x, L1_attn_wq, L1_attn_bq, L1_attn_wk, L1_attn_bk, L1_attn_wv, L1_attn_bv, L1_attn_wl, L1_attn_bl), axis=-1)
    x = _layernorm(x + _L1_ffn_ref(x, L1_ffn_gate_w, L1_ffn_up_w, L1_ffn_down_w, L1_ffn_gate_scale, L1_ffn_up_scale, L1_ffn_down_scale), axis=-1)
    return x

_drawn_inputs = setup_inputs


def setup_inputs(seed=0):
    import zlib

    import numpy as np

    out = dict(_drawn_inputs(seed))
    spreads = {'L0_attn_Wqk_b': (0.0, 0.8), 'L0_attn_Wv_b': (0.0, 0.8), 'L0_attn_Wo_b': (0.0, 0.1)}
    factors = {'L0_attn_Wqk_w': 8.0,
     'L0_attn_Wv_w': 8.0,
     'L0_attn_Wo_w': 8.0,
     'L0_ffn_w1_scale': 6.855,
     'L0_ffn_w3_scale': 6.677,
     'L0_ffn_w2_scale': 8.0,
     'L1_attn_wq': 3.004,
     'L1_attn_bq': 8.0,
     'L1_attn_wk': 2.699,
     'L1_attn_bk': 8.0,
     'L1_attn_bv': 8.0}
    for name, (base, spread) in spreads.items():
        noise = np.random.default_rng([zlib.crc32(name.encode()), seed]).standard_normal(out[name].shape)
        drawn = base * np.exp(spread * noise) if base else spread * noise
        out[name] = jnp.asarray(drawn.astype(out[name].dtype))
    for name, factor in factors.items():
        out[name] = (out[name] * factor).astype(out[name].dtype)
    return out
```

```python
from contextlib import ExitStack

import concourse.bass as bass
from concourse import mybir

P = 128
B, N, D = 2, 512, 512
T = B * N
TILES = T // P
TB = N // P
KC = D // P
H0, E0 = 8, 8
HD0 = H0 * E0
H1, E1 = 32, 16
J0 = 1792 // P
J1 = (1376 + P - 1) // P
LATE = 4
EPS = 1e-5
PARTS = 3
ROWS = PARTS * PARTS * E0
STACK = 96
RAW = 2
RING = 8
UNITS = 3 * J0 + 3 * KC + 3 * J1
U_DOWN0, U_QKV1, U_GU1, U_DOWN1 = 2 * J0, 3 * J0, 3 * J0 + 3 * KC, 3 * J0 + 3 * KC + 2 * J1
RSQRT_SEED = 0x5F3759DF

ALU = mybir.AluOpType
ACT = mybir.ActivationFunctionType
F32, F32R, BF16, I32 = mybir.dt.float32, mybir.dt.float32r, mybir.dt.bfloat16, mybir.dt.int32
AX = mybir.AxisListType


def ring_index(u):
    return u if u < U_QKV1 else u - 3 * KC


def gate_up_order(chunks):
    early = [(j, b) for b in range(B) for j in range(LATE)]
    return early + [(j, b) for j in range(LATE, chunks) for b in range(B)]


GU0, GU1 = gate_up_order(J0), gate_up_order(J1)


def build(nc, xT, x, wqkv, bqkv, wo, eye, eye16, units, unit_scale, b1, ffn1_scale, out):
    with ExitStack() as ctx:
        def sb(name, shape, dt=F32, at=ctx):
            return at.enter_context(nc.sbuf_tensor(name, shape, dt))

        def sem(name):
            return ctx.enter_context(nc.semaphore(name))

        bank = [ctx.enter_context(nc.psum_tensor(f"bank{i}", [P, 512], F32)) for i in range(8)]
        st_bank = [None, None]

        x_tok = sb("x_tok", [P, TILES, D])
        xh = sb("xh", [P, KC, T], F32R)
        xl = sb("xl", [P, KC, T], F32R)
        ring = sb("ring", [P, RING, 2, 512], F32R)
        raw = sb("raw", [P, RAW, 512])
        ident = sb("ident", [P, P])
        ident16 = sb("ident16", [P, P], BF16)
        uscale = sb("uscale", [P, 3 * J0, KC])
        fscale = sb("fscale", [P, 3])
        z = sb("z", [P, D])
        sg = sb("sg", [P, 2, N])
        hf = sb("hf", [P, 2, N])
        stats = sb("stats", [P, 6])
        mv = sb("mv", [P, 2])
        nw = sb("nw", [P, 4])

        s0 = ExitStack()
        QT = [None, None]
        KT = [None, None]
        Qst = [None, None]
        V0 = [None, None]
        QT[0] = sb("QT0", [P, H0, N], BF16, s0)
        KT[0] = sb("KT0", [P, H0, N], BF16, s0)
        Qst[0] = sb("Qst0", [P, TB, H0, STACK], BF16, s0)
        Kst = sb("Kst", [P, TB, H0, STACK], BF16, s0)
        V0[0] = sb("V00", [P, TB, H0, 32], F32, s0)
        QT[1] = sb("QT1", [P, H0, N], BF16, s0)
        KT[1] = sb("KT1", [P, H0, N], BF16, s0)
        Qst[1] = sb("Qst1", [P, TB, H0, STACK], BF16, s0)
        V0[1] = sb("V01", [P, TB, H0, 32], F32, s0)
        w_qkv = sb("w_qkv", [P, KC, 192], F32, s0)
        b_qkv = sb("b_qkv", [P, 192], F32, s0)
        w_o = sb("w_o", [P, D], F32, s0)
        qkv = sb("qkv", [P, TB, 192], F32, s0)
        part = sb("part", [P, PARTS, 2, TB, HD0], BF16, s0)
        rest = sb("rest", [P, 2, TB, HD0], F32, s0)
        smax = sb("smax", [P, TB, H0], F32, s0)
        srest = sb("srest", [P, TB, H0], F32, s0)
        OT = sb("OT", [P, 4, 256], F32, s0)
        o_rec = sb("o_rec", [P, 2, TB, 4], F32, s0)
        o_norm = sb("o_norm", [P, TB, P], F32, s0)
        oT = sb("oT", [P, N], F32, s0)
        with ExitStack() as s0x:
            xT0 = sb("xT0", [P, KC, T], F32, s0x)
        PT = [sb(f"PT{i}", [P, 4, TB, 256], F32, s0) for i in range(2)]
        s0.close()

        with ExitStack() as s1:
            hid0 = sb("hid0", [P, J0, 2, T], F32R, s1)

        with ExitStack() as s2:
            w_qkv1 = sb("w_qkv1", [P, 3, KC, 2, D], F32R, s2)
            bias1 = sb("bias1", [P, 3, D], F32, s2)
            qpad = sb("qpad", [P, H1, 32], F32, s2)
            kpad = sb("kpad", [P, H1, 32], F32, s2)
            qT = sb("qT", [P, 32, H1], F32, s2)
            kT = sb("kT", [P, 32, H1], F32, s2)
            kbd = sb("kbd", [P, 32, 4, H1], F32, s2)
            vs = sb("vs", [P, E1, H1], F32, s2)
            vT = sb("vT", [P, 32, E1], F32, s2)
            vbd = sb("vbd", [P, 32, 4, E1 + 1], F32, s2)
            mx1 = sb("mx1", [P, 32], F32, s2)
            pr = sb("pr", [P, 32, 32], F32, s2)
            prT = sb("prT", [P, 32, 32], F32, s2)
            rec1 = sb("rec1", [P, 32], F32, s2)
            cn = sb("cn", [P, E1, 32], F32, s2)
            ctx1 = sb("ctx1", [P, H1, E1], F32, s2)

        with ExitStack() as s3:
            hid1 = sb("hid1", [P, J1, 2, T], F32R, s3)

        got = {n: sem("got_" + n) for n in
               ("wqkv", "bqkv", "xT0", "xT1", "eye", "x", "wo", "uscale", "fscale", "bias1")}
        raw_in = [sem(f"raw_in{i}") for i in range(RAW)]
        w_ready = sem("w_ready")
        pool_init = sem("pool_init")
        pool_stack = sem("pool_stack")
        pool_v = sem("pool_v")
        pool_pads = sem("pool_pads")
        pool_step = sem("pool_step")
        pe_qkv0 = sem("pe_qkv0")
        pe_T = sem("pe_T")
        pe_S = sem("pe_S")
        pe_W = sem("pe_W")
        pe_ST = sem("pe_ST")
        pe_PV = sem("pe_PV")
        pe_OT = sem("pe_OT")
        pe_oT = sem("pe_oT")
        pe_y = sem("pe_y")
        pe_xT = sem("pe_xT")
        pe_G = sem("pe_G")
        pe_U = sem("pe_U")
        pe_down = sem("pe_down")
        pe_q1, pe_k1, pe_v1 = sem("pe_q1"), sem("pe_k1"), sem("pe_v1")
        pe_S1, pe_C1 = sem("pe_S1"), sem("pe_C1")
        act_T = sem("act_T")
        act_W = sem("act_W")
        act_exp = sem("act_exp")
        act_oT = sem("act_oT")
        act_xh = sem("act_xh")
        act_silu = sem("act_silu")
        act_hh = sem("act_hh")
        act_kbd, act_vbd, act_E1 = sem("act_kbd"), sem("act_vbd"), sem("act_E1")
        dve_qkv0 = sem("dve_qkv0")
        dve_parts = sem("dve_parts")
        dve_T = sem("dve_T")
        dve_max = sem("dve_max")
        dve_mparts = sem("dve_mparts")
        dve_OT = sem("dve_OT")
        dve_on = sem("dve_on")
        dve_z = sem("dve_z")
        dve_xn = sem("dve_xn")
        dve_xl = sem("dve_xl")
        dve_h = sem("dve_h")
        dve_hl = sem("dve_hl")
        dve_qe, dve_ke, dve_ve = sem("dve_qe"), sem("dve_ke"), sem("dve_ve")
        dve_qT, dve_kT, dve_vT = sem("dve_qT"), sem("dve_kT"), sem("dve_vT")
        dve_sub, dve_prT, dve_cn = sem("dve_sub"), sem("dve_prT"), sem("dve_cn")
        dve_step = sem("dve_step")
        out_done = sem("out_done")

        def unit_used(r):
            layer = r >= U_QKV1
            k = r - layer * U_QKV1
            chunks, order, base = (J0, J1)[layer], (GU0, GU1)[layer], layer * len(GU0)
            if k < 2 * chunks:
                return (pe_G, pe_U)[k % 2], base + order.index((k // 2, B - 1)) + 1
            if k - 2 * chunks < chunks - LATE:
                return pe_down, layer * (J0 - LATE) + k - 2 * chunks + 1
            return pe_y, (2 + layer) * TILES

        def st_scores(n):
            return [bank[2 + 2 * (n % 2) + i] for i in range(2)]

        def bank16(i):
            return bank[i][:, :].bitcast(BF16)

        block = ctx.enter_context(nc.Block())

        @block.sync
        def _(sp):
            sp.dma_start(w_qkv[:], wqkv).then_inc(got["wqkv"], 16)
            for b in range(B):
                sp.dma_start(xT0[:, :, b * N:(b + 1) * N], xT[b]).then_inc(got[f"xT{b}"], 16)
            sp.dma_start(b_qkv[:], bqkv.partition_broadcast(P)).then_inc(got["bqkv"], 16)
            sp.dma_start(ident[:], eye).then_inc(got["eye"], 16)
            sp.dma_start(ident16[:], eye16).then_inc(got["eye"], 16)
            sp.dma_start(uscale[:], unit_scale.partition_broadcast(P)).then_inc(got["uscale"], 16)
            sp.dma_start(w_o[:], wo).then_inc(got["wo"], 16)
            sp.dma_start(x_tok[:], x.rearrange("(t p) d -> p t d", p=P)).then_inc(got["x"], 16)
            sp.dma_start(fscale[:], ffn1_scale.partition_broadcast(P)).then_inc(got["fscale"], 16)
            for u in range(UNITS):
                if u >= RAW:
                    sp.wait_ge(w_ready, u - RAW + 1)
                sp.dma_start(raw[:, u % RAW, :], units[u]).then_inc(raw_in[u % RAW], 16)
                if u == U_QKV1 + 3 * KC - 1:
                    sp.wait_ge(pe_y, 2 * TILES)
                    sp.dma_start(bias1[:], b1.partition_broadcast(P)).then_inc(got["bias1"], 16)
            for t in range(TILES):
                sp.wait_ge(dve_xn, 3 * TILES + t + 1)
                sp.dma_start(out[t * P:(t + 1) * P, :], x_tok[:, t, :]).then_inc(out_done, 16)
            sp.wait_ge(out_done, 16 * TILES)

        @block.gpsimd
        def _(pool):
            ms = nc.gpsimd.memset
            steps = [0]

            def step(ins):
                steps[0] += 1
                ins.then_inc(pool_step, 1)
                pool.wait_ge(pool_step, steps[0])

            ms(Kst[:, :, :, ROWS:ROWS + 3], 1.0)
            ms(Kst[:, :, :, ROWS + 3:STACK], 0.0)
            for b in range(B):
                ms(Qst[b][:, :, :, ROWS:STACK], 0.0)
                ms(V0[b][:, :, :, E0:E0 + 1], 1.0)
                ms(V0[b][:, :, :, E0 + 1:], 0.0)
            ms(o_norm[:, :, HD0:HD0 + 1], 1.0)
            step(ms(o_norm[:, :, HD0 + 1:], 0.0))
            for a in (QT[0], KT[0], QT[1]):
                step(ms(a[STACK:P, :, :].bitcast(F32), 0.0))
            ms(KT[1][STACK:P, :, :].bitcast(F32), 0.0).then_inc(pool_init, 1)
            pool.wait_ge(pool_init, 1)
            for b in range(B):
                pool.wait_ge(dve_parts, b + 1)
                if b == 1:
                    pool.wait_ge(pe_T, 4)
                for qk, dst in ((1, Kst), (0, Qst[b])):
                    for a in range(PARTS):
                        src = part[:, a, qk].rearrange("p t (h e) -> p (t h) e", e=E0)
                        rows = dst[:, :, :, 0:ROWS].rearrange("p t h (i j e) -> p (t h) i j e", i=PARTS, j=PARTS)
                        to = rows[:, :, :, a, :] if qk else rows[:, :, a, :, :]
                        last = nc.gpsimd.tensor_copy(to, src.unsqueeze(2).to_broadcast([P, TB * H0, PARTS, E0]))
                    last.then_inc(pool_stack, 1)
                last = nc.gpsimd.tensor_copy(V0[b][:, :, :, 0:E0],
                                             qkv[:, :, 2 * HD0:].rearrange("p t (h e) -> p t h e", e=E0))
                last.then_inc(pool_v, 1)

            pool.wait_ge(got["uscale"], 16)
            for u in range(UNITS):
                if u == U_GU1:
                    pool.wait_ge(pe_y, 2 * TILES)
                    ms(qpad[:, :, E1:], 0.0)
                    ms(kpad[:, :, E1:], 0.0).then_inc(pool_pads, 1)
                    ms(kbd[:], 0.0)
                    ms(vbd[:, :, :, 0:E1], 0.0)
                    step(ms(vbd[:, :, :, E1:], 0.0))
                    for g in range(3):
                        step(ms(vbd[32 * g:32 * g + 32, :, g, E1:], 1.0))
                    ms(vbd[96:P, :, 3, E1:], 1.0).then_inc(pool_pads, 1)
                    pool.wait_ge(pool_pads, 2)
                w = raw[:, u % RAW, :]
                if U_QKV1 <= u < U_GU1:
                    k = u - U_QKV1
                    dst = w_qkv1[:, k // KC, k % KC]
                    if k % 2 == 0:
                        pool.wait_ge(pe_down, k // 2 + 1)
                else:
                    r = ring_index(u)
                    dst = ring[:, r % RING]
                    if r >= RING:
                        pool.wait_ge(*unit_used(r - RING))
                pool.wait_ge(raw_in[u % RAW], 16 * (u // RAW + 1))
                if u < U_QKV1:
                    step(nc.gpsimd.tensor_tensor(
                        w.rearrange("p (c m) -> p c m", c=KC), w.rearrange("p (c m) -> p c m", c=KC),
                        uscale[:, u, :].unsqueeze(2).to_broadcast([P, KC, P]), ALU.mult))
                step(nc.gpsimd.tensor_copy(dst[:, 0, :], w))
                nc.gpsimd.tensor_tensor(dst[:, 1, :], w, dst[:, 0, :].bitcast(F32), ALU.subtract).then_inc(w_ready, 1)

        @block.tensor
        def _(pe):
            def split_product(psum, sh, sl, mh, ml, first, last):
                nc.tensor.matmul(psum, sh, mh, start=first, stop=False)
                nc.tensor.matmul(psum, sh, ml, start=False, stop=False)
                return nc.tensor.matmul(psum, sl, mh, start=False, stop=last)

            def project0(t):
                if t == 0:
                    pe.wait_ge(got["wqkv"], 16)
                if t % TB == 0:
                    pe.wait_ge(got[f"xT{t // TB}"], 16)
                if t >= 2:
                    pe.wait_ge(dve_qkv0, t - 1)
                for c in range(KC):
                    mm = nc.tensor.matmul(bank[t % 2][:, 0:192], xT0[:, c, t * P:(t + 1) * P], w_qkv[:, c, :],
                                          start=(c == 0), stop=(c == KC - 1))
                mm.then_inc(pe_qkv0, 1)

            def transpose_stack(b):
                if b == 0:
                    pe.wait_ge(got["eye"], 32)
                for i in range(8):
                    n = 8 * b + i
                    pe.wait_ge(pool_stack, 2 * b + 1 + i // 4)
                    if n >= 6:
                        pe.wait_ge(act_T if n % 2 == 0 else dve_T, (n - 6) // 2 + 1)
                    src = Kst if i < 4 else Qst[b]
                    for hh in range(2):
                        for t in range(TB):
                            c = hh * N + t * P
                            mm = nc.tensor.transpose(bank16(2 + n % 6)[0:STACK, c:c + P],
                                                     src[:, t, 2 * (i % 4) + hh, :], ident16[:])
                    mm.then_inc(pe_T, 1)

            def scores_for_max(b, h):
                for t in range(TB):
                    n = (b * H0 + h) * TB + t
                    if h == 0 and t == 0:
                        pe.wait_ge(pool_init, 1)
                        pe.wait_ge(act_T, 4 * b + 4)
                        pe.wait_ge(dve_T, 4 * b + 4)
                    if n >= 2:
                        pe.wait_ge(dve_max, n - 1)
                    if b == 1 and h == 0 and t == 0:
                        pe.wait_ge(act_W, 4)
                    nc.tensor.matmul(bank[n % 2][:], QT[b][:, h, t * P:(t + 1) * P], KT[b][:, h, :],
                                     start=True, stop=True).then_inc(pe_S, 1)

            def transpose_max(b):
                pe.wait_ge(dve_mparts, b + 1)
                for i in range(4):
                    n = 4 * b + i
                    if i >= 2:
                        pe.wait_ge(act_W, n - 1)
                    for hh in range(2):
                        for t in range(TB):
                            c = hh * N + t * P
                            mm = nc.tensor.transpose(bank16(n % 2)[64:STACK, c:c + P],
                                                     Qst[b][:, t, 2 * i + hh, 64:STACK], ident16[:])
                    mm.then_inc(pe_W, 1)

            def scores_transposed(u):
                b, g, half = u // 4, u // 2 % 2, u % 2
                if u % 4 == 0:
                    pe.wait_ge(act_W, 4 * b + 4)
                for i in range(4):
                    n = 4 * u + i
                    if n == 0:
                        pe.wait_ge(act_T, 8)
                        pe.wait_ge(dve_T, 8)
                    if n >= 2:
                        pe.wait_ge(act_exp, n - 1)
                    for kt in range(TB):
                        mm = nc.tensor.matmul(
                            st_scores(n)[kt // 2][:, (kt % 2) * 256:(kt % 2) * 256 + 256],
                            KT[b][:, 4 * g + i, kt * P:(kt + 1) * P],
                            QT[b][:, 4 * g + i, half * 256:(half + 1) * 256], start=True, stop=True)
                    mm.then_inc(pe_ST, 1)

            def weigh_values(u):
                b, g = u // 4, u // 2 % 2
                pe.wait_ge(act_exp, 4 * u + 4)
                pe.wait_ge(pool_v, b + 1)
                if u >= 2:
                    pe.wait_ge(dve_OT, u - 1)
                for kt in range(TB):
                    for i in range(4):
                        mm = nc.tensor.matmul(bank[6 + u % 2][32 * i:32 * i + 32, 0:256],
                                              V0[b][:, kt, 4 * g + i, :], PT[u % 2][:, i, kt, :],
                                              start=(kt == 0), stop=(kt == TB - 1), skip_group_check=True)
                mm.then_inc(pe_PV, 1)

            def output_to_tokens(b):
                pe.wait_ge(dve_OT, 4 * b + 4)
                if b == 0:
                    pe.wait_ge(act_W, 8)
                if b == 1:
                    pe.wait_ge(dve_xl, TB)
                for g in range(2):
                    for t in range(TB):
                        mm = nc.tensor.transpose(bank[g][:, t * P:(t + 1) * P],
                                                 OT[:, 2 * g + t // 2, (t % 2) * P:(t % 2) * P + P], ident[:])
                    mm.then_inc(pe_OT, 1)

            def output_to_features(b):
                pe.wait_ge(dve_on, 2 * b + 2)
                pe.wait_ge(pool_init, 1)
                for t in range(TB):
                    mm = nc.tensor.transpose(bank[0][:, t * P:(t + 1) * P], o_norm[:, t, :], ident[:])
                mm.then_inc(pe_oT, 1)

            def output_product(t):
                if t % TB == 0:
                    pe.wait_ge(act_oT, t // TB + 1)
                if t == 0:
                    pe.wait_ge(got["wo"], 16)
                if t % TB >= 2:
                    pe.wait_ge(dve_xl, t - 1)
                c = (t % TB) * P
                nc.tensor.matmul(bank[t % 2][:], oT[:, c:c + P], w_o[:], start=True, stop=True).then_inc(pe_y, 1)

            def transpose_x(layer, t, to):
                n = layer * TILES + t
                pe.wait_ge(dve_xn, n + 1)
                if layer == 2 and t > 0:
                    pe.wait_ge(dve_xl, n)
                for c in range(KC):
                    mm = nc.tensor.transpose(bank[to][:, c * P:(c + 1) * P], x_tok[:, t, c * P:(c + 1) * P], ident[:])
                mm.then_inc(pe_xT, 1)

            def gate_up(layer, k):
                j, b = (GU0, GU1)[layer][k]
                kk = k + layer * len(GU0)
                u = (0, U_GU1)[layer] + 2 * j
                if j == 0:
                    ready = (0, 2 * TILES)[layer] + TB * (b + 1)
                    pe.wait_ge(dve_xl, ready)
                if k == 0 and layer == 0:
                    pe.wait_ge(act_exp, 4 * 8)
                if k == 0 and layer == 1:
                    pe.wait_ge(dve_ke, TILES)
                for what, psum, done, free in ((0, bank[(2, 0)[layer]], pe_G, act_silu),
                                               (1, bank[(3, 1)[layer]], pe_U, dve_h)):
                    pe.wait_ge(w_ready, u + what + 1)
                    if kk >= 1:
                        pe.wait_ge(free, kk)
                    w = ring[:, ring_index(u + what) % RING].rearrange("p s (c m) -> p s c m", c=KC)
                    cols = slice(b * N, (b + 1) * N)
                    for c in range(KC):
                        mm = split_product(psum[:], w[:, 0, c, :], w[:, 1, c, :], xh[:, c, cols], xl[:, c, cols],
                                           c == 0, c == KC - 1)
                    mm.then_inc(done, 1)

            def down_chunk(layer, j, t):
                chunks = (J0, J1)[layer]
                hid = (hid0, hid1)[layer]
                w = ring[:, ring_index((U_DOWN0, U_DOWN1)[layer] + j) % RING]
                cols = slice(t * P, (t + 1) * P)
                return split_product(bank[t][:], hid[:, j, 0, cols], hid[:, j, 1, cols], w[:, 0, :], w[:, 1, :],
                                     j == 0, j == chunks - 1)

            def down(layer, between):
                chunks = (J0, J1)[layer]
                base = layer * len(GU0)
                order = ([6, 7, 0, 1, 4, 5, 2, 3], [2, 3, 4, 5, 6, 7, 0, 1])[layer]
                for j in range(chunks - LATE):
                    pe.wait_ge(w_ready, (U_DOWN0, U_DOWN1)[layer] + j + 1)
                    pe.wait_ge(dve_hl, base + max(k for k, x in enumerate((GU0, GU1)[layer]) if x[0] == j) + 1)
                    for t in order:
                        if j == 0 and t == order[-2]:
                            pe.wait_ge(act_silu, base + 2 * chunks)
                        if j == 0 and t == order[-1]:
                            pe.wait_ge(dve_h, base + 2 * chunks)
                        mm = down_chunk(layer, j, t)
                    mm.then_inc(pe_down, 1)
                pe.wait_ge(dve_hl, base + 2 * chunks)
                pe.wait_ge(w_ready, (U_DOWN0, U_DOWN1)[layer] + chunks)
                for t in range(TILES):
                    for j in range(chunks - LATE, chunks):
                        mm = down_chunk(layer, j, t)
                    mm.then_inc(pe_y, 1)
                    between(t)

            def project1(t):
                cols = slice(t * P, (t + 1) * P)
                if t == 0:
                    pe.wait_ge(w_ready, U_GU1)
                pe.wait_ge(dve_xl, TILES + t + 1)
                if t == 0:
                    pe.wait_ge(dve_xl, TILES + 3)
                for i, (done, free) in enumerate(((pe_q1, dve_qe), (pe_k1, dve_ke), (pe_v1, dve_ve))):
                    if t:
                        pe.wait_ge(free, t)
                    for c in range(KC):
                        sh, sl = xh[:, c, cols], xl[:, c, cols]
                        mm = split_product(bank[i][:], sh, sl, w_qkv1[:, i, c, 0, :], w_qkv1[:, i, c, 1, :],
                                           c == 0, c == KC - 1)
                    mm.then_inc(done, 1)

            def scores1(t):
                pe.wait_ge(dve_qT, t + 1)
                pe.wait_ge(act_kbd, t + 1)
                if t == 0:
                    pe.wait_ge(dve_xl, TILES + 6)
                if t:
                    pe.wait_ge(dve_sub, t)
                for s in range(8):
                    for j in range(4):
                        i = 4 * s + j
                        mm = nc.tensor.matmul(bank[4 + s // 4][32 * j:32 * j + 32, (s % 4) * P:(s % 4 + 1) * P],
                                              qT[:, i, :], kbd[:, i, :, :], start=True, stop=True,
                                              skip_group_check=True)
                mm.then_inc(pe_S1, 1)

            def context1(t):
                pe.wait_ge(dve_prT, t + 1)
                pe.wait_ge(act_vbd, t + 1)
                if t == 0:
                    pe.wait_ge(dve_xl, 2 * TILES)
                    pe.wait_ge(pool_pads, 2)
                if t:
                    pe.wait_ge(dve_cn, t)
                W = 4 * (E1 + 1)
                for s in range(8):
                    for g in range(4):
                        mm = nc.tensor.matmul(bank[6 + s // 4][32 * g:32 * g + 32, (s % 4) * W:(s % 4 + 1) * W],
                                              prT[:, 4 * s + g, :], vbd[:, 4 * s + g, :, :], start=True, stop=True,
                                              skip_group_check=True)
                mm.then_inc(pe_C1, 1)

            for t in range(TILES):
                project0(t)
            transpose_stack(0)
            for h in range(H0):
                scores_for_max(0, h)
                if h == 1:
                    transpose_stack(1)
            transpose_max(0)
            for u in range(4):
                scores_transposed(u)
                for h in (2 * u, 2 * u + 1):
                    scores_for_max(1, h)
                weigh_values(u)
            transpose_max(1)
            scores_transposed(4)
            output_to_tokens(0)
            weigh_values(4)
            scores_transposed(5)
            output_to_features(0)
            weigh_values(5)
            output_product(0)
            output_product(1)
            scores_transposed(6)
            weigh_values(6)
            transpose_x(0, 0, 0)
            output_product(2)
            transpose_x(0, 1, 1)
            output_product(3)
            scores_transposed(7)
            weigh_values(7)
            transpose_x(0, 2, 0)
            transpose_x(0, 3, 1)
            output_to_tokens(1)
            gate_up(0, 0)
            output_to_features(1)
            output_product(4)
            output_product(5)
            gate_up(0, 1)
            transpose_x(0, 4, 0)
            output_product(6)
            transpose_x(0, 5, 1)
            output_product(7)
            gate_up(0, 2)
            transpose_x(0, 6, 0)
            transpose_x(0, 7, 1)
            for k in range(3, len(GU0)):
                gate_up(0, k)

            down(0, lambda t: transpose_x(1, t - 2, t - 2) if t >= 2 else None)
            for t in range(TILES):
                project1(t)
                if t == 0:
                    transpose_x(1, 6, 6)
                    transpose_x(1, 7, 7)
                if t >= 1:
                    scores1(t - 1)
                if t >= 2:
                    context1(t - 2)
                if t >= 3:
                    transpose_x(2, t - 3, 3)
            gate_up(1, 0)
            scores1(7)
            context1(6)
            transpose_x(2, 5, 3)
            gate_up(1, 1)
            context1(7)
            transpose_x(2, 6, 3)
            gate_up(1, 2)
            transpose_x(2, 7, 3)
            for k in range(3, len(GU1)):
                gate_up(1, k)
            down(1, lambda t: None)

        @block.scalar
        def _(act):
            def evacuate_stack(b):
                for n in range(8 * b, 8 * b + 8, 2):
                    act.wait_ge(pe_T, n + 1)
                    i = n % 8
                    dst = (KT if i < 4 else QT)[b][0:STACK, 2 * (i % 4):2 * (i % 4) + 2, :]
                    nc.scalar.copy(dst, bank16(2 + n % 6)[0:STACK, :].rearrange("p (h n) -> p h n", h=2)).then_inc(act_T, 1)

            def evacuate_max(b):
                for n in range(4 * b, 4 * b + 4):
                    act.wait_ge(pe_W, n + 1)
                    i = n % 4
                    nc.scalar.copy(QT[b][64:STACK, 2 * i:2 * i + 2, :],
                                   bank16(n % 2)[64:STACK, :].rearrange("p (h n) -> p h n", h=2)).then_inc(act_W, 1)

            def exponentials(u):
                if u >= 2:
                    act.wait_ge(pe_PV, u - 1)
                for i in range(4):
                    n = 4 * u + i
                    act.wait_ge(pe_ST, n + 1)
                    for hf_ in range(2):
                        ins = nc.scalar.activation(PT[u % 2][:, i, 2 * hf_:2 * hf_ + 2, :],
                                                   st_scores(n)[hf_][:].rearrange("p (k n) -> p k n", k=2), ACT.Exp)
                    ins.then_inc(act_exp, 1)

            def evacuate_oT(b):
                act.wait_ge(pe_oT, b + 1)
                nc.scalar.copy(oT[:], bank[0][:]).then_inc(act_oT, 1)

            def x_hi(n, bk):
                act.wait_ge(pe_xT, n + 1)
                t = n % TILES
                nc.scalar.copy(xh[:, :, t * P:(t + 1) * P],
                               bank[bk][:].rearrange("p (c n) -> p c n", c=KC)).then_inc(act_xh, 1)

            def hidden(layer, k):
                kk = k + layer * len(GU0)
                j, b = (GU0, GU1)[layer][k]
                act.wait_ge(pe_G, kk + 1)
                if kk >= 2:
                    act.wait_ge(dve_h, kk - 1)
                if layer and k == 0:
                    act.wait_ge(got["fscale"], 16)
                nc.scalar.activation(sg[:, kk % 2, :], bank[(2, 0)[layer]][:], ACT.Silu,
                                     scale=fscale[:, 0:1] if layer else 1.0).then_inc(act_silu, 1)
                act.wait_ge(dve_h, kk + 1)
                nc.scalar.copy((hid0, hid1)[layer][:, j, 0, b * N:(b + 1) * N], hf[:, kk % 2, :]).then_inc(act_hh, 1)

            evacuate_stack(0)
            evacuate_stack(1)
            evacuate_max(0)
            for u in range(4):
                exponentials(u)
            evacuate_max(1)
            exponentials(4)
            exponentials(5)
            evacuate_oT(0)
            exponentials(6)
            x_hi(0, 0)
            x_hi(1, 1)
            exponentials(7)
            x_hi(2, 0)
            x_hi(3, 1)
            hidden(0, 0)
            evacuate_oT(1)
            hidden(0, 1)
            x_hi(4, 0)
            x_hi(5, 1)
            hidden(0, 2)
            x_hi(6, 0)
            x_hi(7, 1)
            for k in range(3, len(GU0)):
                hidden(0, k)
            for t in range(TILES):
                x_hi(TILES + t, t)

            def k_blocks(t):
                act.wait_ge(dve_kT, t + 1)
                if t == 0:
                    act.wait_ge(pool_pads, 2)
                else:
                    act.wait_ge(pe_S1, t)
                for g in range(4):
                    rows = slice(32 * g, 32 * g + 32)
                    ins = nc.scalar.copy(kbd[rows, :, g, :], kT[rows])
                ins.then_inc(act_kbd, 1)

            def v_blocks(t):
                act.wait_ge(dve_vT, t + 1)
                if t == 0:
                    act.wait_ge(pool_pads, 2)
                else:
                    act.wait_ge(pe_C1, t)
                for j in range(4):
                    to = vbd[32 * j:32 * j + 32].rearrange("p (s g) i e -> p s g i e", g=4)
                    for g in range(4):
                        ins = nc.scalar.copy(to[:, :, g, j, 0:E1],
                                             vT[32 * g:32 * g + 32].rearrange("p (s i) e -> p s i e", i=4)[:, :, j, :])
                ins.then_inc(act_vbd, 1)

            def exp1(t):
                act.wait_ge(dve_sub, t + 1)
                nc.scalar.activation(pr[:], pr[:], ACT.Exp, scale=E1 ** -0.5).then_inc(act_E1, 1)

            for t in range(TILES):
                if t >= 1:
                    exp1(t - 1)
                k_blocks(t)
                if t >= 1:
                    v_blocks(t - 1)
                if t >= 3:
                    x_hi(2 * TILES + t - 3, 3)
            hidden(1, 0)
            exp1(7)
            v_blocks(7)
            x_hi(2 * TILES + 5, 3)
            hidden(1, 1)
            x_hi(2 * TILES + 6, 3)
            hidden(1, 2)
            x_hi(2 * TILES + 7, 3)
            for k in range(3, len(GU1)):
                hidden(1, k)

        @block.vector
        def _(dve):
            tt, ts = nc.vector.tensor_tensor, nc.vector.tensor_scalar
            steps = [0]

            def step(ins):
                steps[0] += 1
                ins.then_inc(dve_step, 1)
                dve.wait_ge(dve_step, steps[0])

            def evacuate_qkv(t):
                if t == 0:
                    dve.wait_ge(got["bqkv"], 16)
                if t == TB:
                    dve.wait_ge(pool_v, 1)
                dve.wait_ge(pe_qkv0, t + 1)
                tt(qkv[:, t % TB, :], bank[t % 2][:, 0:192], b_qkv[:], ALU.add).then_inc(dve_qkv0, 1)

            def split_qk(b):
                dve.wait_ge(dve_qkv0, TB * (b + 1))
                if b:
                    dve.wait_ge(dve_parts, 1)
                    dve.wait_ge(pool_stack, 2)
                qk = qkv[:, :, 0:2 * HD0].rearrange("p t (q x) -> p q t x", q=2)
                step(nc.vector.tensor_copy(part[:, 0], qk))
                step(tt(rest[:], qk, part[:, 0], ALU.subtract))
                step(nc.vector.tensor_copy(part[:, 1], rest[:]))
                step(tt(rest[:], rest[:], part[:, 1], ALU.subtract))
                nc.vector.tensor_copy(part[:, 2], rest[:]).then_inc(dve_parts, 1)

            def evacuate_stack(b):
                for n in range(8 * b + 1, 8 * b + 8, 2):
                    dve.wait_ge(pe_T, n + 1)
                    i = n % 8
                    dst = (KT if i < 4 else QT)[b][0:STACK, 2 * (i % 4):2 * (i % 4) + 2, :]
                    nc.vector.tensor_copy(dst, bank16(2 + n % 6)[0:STACK, :].rearrange("p (h n) -> p h n", h=2)).then_inc(dve_T, 1)

            def maxima(b, h):
                if b == 1 and h == 0:
                    dve.wait_ge(dve_mparts, 1)
                for t in range(TB):
                    n = (b * H0 + h) * TB + t
                    dve.wait_ge(pe_S, n + 1)
                    nc.vector.tensor_reduce(smax[:, t, h:h + 1], bank[n % 2][:], AX.X, ALU.max,
                                            negate=True).then_inc(dve_max, 1)

            def split_max(b):
                dve.wait_ge(dve_max, 32 * (b + 1))
                if b:
                    dve.wait_ge(dve_mparts, 1)
                if b == 0:
                    dve.wait_ge(pool_init, 1)
                to = [Qst[b][:, :, :, ROWS + a] for a in range(PARTS)]
                step(nc.vector.tensor_copy(to[0], smax[:]))
                step(tt(srest[:], smax[:], to[0], ALU.subtract))
                step(nc.vector.tensor_copy(to[1], srest[:]))
                step(tt(srest[:], srest[:], to[1], ALU.subtract))
                nc.vector.tensor_copy(to[2], srest[:]).then_inc(dve_mparts, 1)

            def evacuate_output(u):
                dve.wait_ge(pe_PV, u + 1)
                nc.vector.tensor_copy(OT[:, u % 4, :], bank[6 + u % 2][:, 0:256]).then_inc(dve_OT, 1)

            def normalise_output(b):
                if b == 0:
                    dve.wait_ge(pool_init, 1)
                else:
                    dve.wait_ge(dve_on, 2)
                    dve.wait_ge(pe_oT, 1)
                for g in range(2):
                    dve.wait_ge(pe_OT, 2 * b + g + 1)
                    o = bank[g][:].rearrange("p (t h e) -> p t h e", t=TB, h=4)
                    step(nc.vector.reciprocal(o_rec[:, g], o[:, :, :, E0]))
                    nc.vector.scalar_tensor_tensor(
                        out=o_norm[:, :, g * 32:(g + 1) * 32].rearrange("p t (h e) -> p t h e", h=4),
                        in0=o[:, :, :, 0:E0], scalar=HD0 ** -0.5,
                        in1=o_rec[:, g].unsqueeze(3).to_broadcast([P, TB, 4, E0]),
                        op0=ALU.mult, op1=ALU.mult).then_inc(dve_on, 1)

            def x_lo(n, bk):
                dve.wait_ge(act_xh, n + 1)
                t = n % TILES
                tt(xl[:, :, t * P:(t + 1) * P], bank[bk][:].rearrange("p (c n) -> p c n", c=KC),
                   xh[:, :, t * P:(t + 1) * P].bitcast(F32), ALU.subtract).then_inc(dve_xl, 1)

            def layernorm(n, src):
                layer, t = divmod(n, TILES)
                xt, zz = x_tok[:, t, :], z[:]
                if layer != 2:
                    dve.wait_ge(pe_y, n + 1 - (TILES if layer == 3 else 0))
                if n == 0:
                    dve.wait_ge(got["x"], 16)
                else:
                    dve.wait_ge(dve_xn, n)
                if layer == 3:
                    ins = nc.vector.scalar_tensor_tensor(out=zz, in0=src, scalar=fscale[:, 2:3], in1=xt,
                                                         op0=ALU.mult, op1=ALU.add)
                else:
                    ins = tt(zz, src, xt, ALU.add)
                ins.then_inc(dve_z, 1)
                dve.wait_ge(dve_z, n + 1)
                step(nc.vector.bn_stats(stats[:], zz))
                step(nc.vector.bn_aggr(mv[:], stats[:]))
                v, y, a = nw[:, 0:1], nw[:, 1:2], nw[:, 2:3]
                step(ts(v, mv[:, 1:2], EPS, None, ALU.add))
                step(ts(a.bitcast(I32), v.bitcast(I32), 1, None, ALU.logical_shift_right))
                step(ts(y.bitcast(I32), a.bitcast(I32), -1.0, float(RSQRT_SEED), ALU.mult, ALU.add))
                for _ in range(3):
                    step(nc.vector.scalar_tensor_tensor(out=a, in0=y, scalar=v, in1=y, op0=ALU.mult, op1=ALU.mult))
                    step(ts(a, a, -0.5, 1.5, ALU.mult, ALU.add))
                    step(tt(y, y, a, ALU.mult))
                ts(xt, zz, mv[:, 0:1], y, ALU.subtract, ALU.mult).then_inc(dve_xn, 1)

            def hidden(layer, k):
                kk = k + layer * len(GU0)
                j, b = (GU0, GU1)[layer][k]
                dve.wait_ge(act_silu, kk + 1)
                dve.wait_ge(pe_U, kk + 1)
                if kk >= 2:
                    dve.wait_ge(dve_hl, kk - 1)
                h = hf[:, kk % 2, :]
                if layer == 0:
                    tt(h, bank[3][:], sg[:, kk % 2, :], ALU.mult).then_inc(dve_h, 1)
                else:
                    if k == 0:
                        dve.wait_ge(got["fscale"], 16)
                    nc.vector.scalar_tensor_tensor(out=h, in0=bank[1][:], scalar=fscale[:, 1:2], in1=sg[:, kk % 2, :],
                                                   op0=ALU.mult, op1=ALU.mult).then_inc(dve_h, 1)
                dve.wait_ge(act_hh, kk + 1)
                hid = (hid0, hid1)[layer]
                tt(hid[:, j, 1, b * N:(b + 1) * N], h, hid[:, j, 0, b * N:(b + 1) * N].bitcast(F32),
                   ALU.subtract).then_inc(dve_hl, 1)

            for t in range(TB):
                evacuate_qkv(t)
            split_qk(0)
            for t in range(TB, TILES):
                evacuate_qkv(t)
            evacuate_stack(0)
            split_qk(1)
            maxima(0, 0)
            maxima(0, 1)
            evacuate_stack(1)
            for h in range(2, H0):
                maxima(0, h)
            split_max(0)
            for u in range(4):
                maxima(1, 2 * u)
                maxima(1, 2 * u + 1)
                evacuate_output(u)
            split_max(1)
            normalise_output(0)
            evacuate_output(4)
            evacuate_output(5)
            layernorm(0, bank[0][:])
            layernorm(1, bank[1][:])
            evacuate_output(6)
            x_lo(0, 0)
            x_lo(1, 1)
            layernorm(2, bank[0][:])
            layernorm(3, bank[1][:])
            evacuate_output(7)
            x_lo(2, 0)
            x_lo(3, 1)
            normalise_output(1)
            hidden(0, 0)
            layernorm(4, bank[0][:])
            layernorm(5, bank[1][:])
            hidden(0, 1)
            x_lo(4, 0)
            x_lo(5, 1)
            layernorm(6, bank[0][:])
            layernorm(7, bank[1][:])
            hidden(0, 2)
            x_lo(6, 0)
            x_lo(7, 1)
            for k in range(3, len(GU0)):
                hidden(0, k)
            for t in range(TILES):
                layernorm(TILES + t, bank[t][:])
                if t >= 2:
                    x_lo(TILES + t - 2, t - 2)

            def evacuate1(t):
                if t == 0:
                    dve.wait_ge(got["bias1"], 16)
                    dve.wait_ge(pool_pads, 1)
                else:
                    dve.wait_ge(dve_kT, t)
                    dve.wait_ge(dve_vT, t)
                for i, (seen, done) in enumerate(((pe_q1, dve_qe), (pe_k1, dve_ke), (pe_v1, dve_ve))):
                    dve.wait_ge(seen, t + 1)
                    to = (qpad[:, :, 0:E1], kpad[:, :, 0:E1], vs[:].rearrange("p e h -> p h e"))[i]
                    tt(to, bank[i][:].rearrange("p (h e) -> p h e", e=E1),
                       bias1[:, i, :].rearrange("p (h e) -> p h e", e=E1), ALU.add).then_inc(done, 1)

            def turn_qk(t):
                dve.wait_ge(dve_ke, t + 1)
                if t:
                    dve.wait_ge(pe_S1, t)
                nc.vector.transpose(qT[:].rearrange("p i h -> p h i"), qpad[:]).then_inc(dve_qT, 1)
                if t:
                    dve.wait_ge(act_kbd, t)
                nc.vector.transpose(kT[:].rearrange("p i h -> p h i"), kpad[:]).then_inc(dve_kT, 1)

            def turn_v(t):
                dve.wait_ge(dve_ve, t + 1)
                if t:
                    dve.wait_ge(act_vbd, t)
                nc.vector.transpose(vT[:].rearrange("p i e -> p e i"), vs[:]).then_inc(dve_vT, 1)

            def softmax1(t):
                dve.wait_ge(pe_S1, t + 1)
                if t:
                    dve.wait_ge(dve_sub, t)
                    dve.wait_ge(dve_prT, t)
                s = [bank[4 + i][:].rearrange("p (i h) -> p i h", h=H1) for i in range(2)]
                for i in range(2):
                    ins = nc.vector.tensor_reduce(mx1[:, 16 * i:16 * i + 16], s[i], AX.X, ALU.max)
                step(ins)
                for i in range(2):
                    ins = tt(pr[:, 16 * i:16 * i + 16, :], s[i],
                             mx1[:, 16 * i:16 * i + 16].unsqueeze(2).to_broadcast([P, 16, H1]), ALU.subtract)
                ins.then_inc(dve_sub, 1)

            def turn_probs(t):
                dve.wait_ge(act_E1, t + 1)
                if t:
                    dve.wait_ge(pe_C1, t)
                nc.vector.transpose(prT[:], pr[:]).then_inc(dve_prT, 1)

            def context_norm(t):
                dve.wait_ge(pe_C1, t + 1)
                if t:
                    dve.wait_ge(dve_cn, t)
                c = [bank[6 + i][:, 0:16 * (E1 + 1)].rearrange("p (i e) -> p i e", e=E1 + 1) for i in range(2)]
                for i in range(2):
                    ins = nc.vector.reciprocal(rec1[:, 16 * i:16 * i + 16], c[i][:, :, E1])
                step(ins)
                for i in range(2):
                    ins = tt(cn[:, :, 16 * i:16 * i + 16].rearrange("p e i -> p i e"), c[i][:, :, 0:E1],
                             rec1[:, 16 * i:16 * i + 16].unsqueeze(2).to_broadcast([P, 16, E1]), ALU.mult)
                ins.then_inc(dve_cn, 1)
                dve.wait_ge(dve_cn, t + 1)
                step(nc.vector.transpose(ctx1[:].rearrange("p h e -> p e h"), cn[:]))
                layernorm(2 * TILES + t, ctx1[:].rearrange("p h e -> p (h e)"))

            for t in range(TILES):
                evacuate1(t)
                if t == 0:
                    x_lo(TILES + 6, 6)
                    x_lo(TILES + 7, 7)
                if t >= 1:
                    softmax1(t - 1)
                turn_qk(t)
                if t >= 1:
                    turn_probs(t - 1)
                if t >= 2:
                    context_norm(t - 2)
                turn_v(t)
                if t >= 3:
                    x_lo(2 * TILES + t - 3, 3)
            hidden(1, 0)
            softmax1(7)
            turn_probs(7)
            context_norm(6)
            x_lo(2 * TILES + 5, 3)
            hidden(1, 1)
            context_norm(7)
            x_lo(2 * TILES + 6, 3)
            hidden(1, 2)
            x_lo(2 * TILES + 7, 3)
            for k in range(3, len(GU1)):
                hidden(1, k)
            for t in range(TILES):
                layernorm(3 * TILES + t, bank[t][:])


def kernel(L0_attn_x, L0_attn_Wqk_w, L0_attn_Wqk_b, L0_attn_Wv_w, L0_attn_Wv_b, L0_attn_Wo_w, L0_attn_Wo_b,
           L0_ffn_w1, L0_ffn_w1_scale, L0_ffn_w3, L0_ffn_w3_scale, L0_ffn_w2, L0_ffn_w2_scale,
           L1_attn_wq, L1_attn_bq, L1_attn_wk, L1_attn_bk, L1_attn_wv, L1_attn_bv, L1_attn_wl, L1_attn_bl,
           L1_ffn_gate_w, L1_ffn_up_w, L1_ffn_down_w, L1_ffn_gate_scale, L1_ffn_up_scale, L1_ffn_down_scale):
    import numpy as np
    from concourse import bacc
    from concourse.bass_utils import run_bass_kernel_spmd
    import ml_dtypes

    f = np.float32
    x = np.asarray(L0_attn_x).reshape(T, D)
    wqk, bqk = np.asarray(L0_attn_Wqk_w), np.asarray(L0_attn_Wqk_b)

    def chunked(w):
        return w.reshape(-1, P, w.shape[1]).transpose(1, 0, 2)

    def columns(w, chunks):
        w = np.asarray(w)
        full = np.zeros((chunks * P, w.shape[1]), f)
        full[:w.shape[0]] = w
        return full.reshape(chunks, P, KC, P).transpose(0, 3, 2, 1).reshape(chunks, P, 512)

    def rows(w, chunks):
        w = np.asarray(w)
        full = np.zeros((chunks * P, w.shape[0]), f)
        full[:w.shape[1]] = w.T
        return full.reshape(chunks, P, w.shape[0])

    def paired(a, b):
        return np.stack([a, b], 1).reshape(-1, P, 512)

    units = np.concatenate([
        paired(columns(L0_ffn_w1, J0), columns(L0_ffn_w3, J0)), rows(L0_ffn_w2, J0),
        rows(L1_attn_wq, KC), rows(L1_attn_wk, KC), rows(L1_attn_wv, KC),
        paired(columns(L1_ffn_gate_w, J1), columns(L1_ffn_up_w, J1)), rows(L1_ffn_down_w, J1)])
    unit_scale = np.concatenate([
        np.stack([np.asarray(L0_ffn_w1_scale), np.asarray(L0_ffn_w3_scale)], 1).reshape(2 * J0, KC),
        np.asarray(L0_ffn_w2_scale).T])
    wo = np.zeros((P, D), f)
    wo[:HD0] = np.asarray(L0_attn_Wo_w).T
    wo[HD0] = np.asarray(L0_attn_Wo_b)
    arrays = {
        "xT": x.reshape(B, N, KC, P).transpose(0, 3, 2, 1),
        "x": x,
        "wqkv": chunked(np.concatenate([wqk[0::2], wqk[1::2], np.asarray(L0_attn_Wv_w)]).T),
        "bqkv": np.concatenate([bqk[0::2], bqk[1::2], np.asarray(L0_attn_Wv_b)]),
        "wo": wo,
        "eye": np.eye(P, dtype=f),
        "eye16": np.eye(P, dtype=ml_dtypes.bfloat16),
        "units": units,
        "unit_scale": unit_scale,
        "b1": np.stack([np.asarray(L1_attn_bq), np.asarray(L1_attn_bk), np.asarray(L1_attn_bv)]),
        "ffn1_scale": np.stack([np.asarray(L1_ffn_gate_scale), np.asarray(L1_ffn_up_scale),
                                np.asarray(L1_ffn_down_scale)]),
    }
    arrays = {k: np.ascontiguousarray(v) for k, v in arrays.items()}
    nc = bacc.Bacc("TRN2", target_bir_lowering=False, num_devices=1)
    aps = {k: nc.dram_tensor(k, v.shape, mybir.dt.from_np(v.dtype), kind="ExternalInput").ap()
           for k, v in arrays.items()}
    out = nc.dram_tensor("out", (T, D), F32, kind="ExternalOutput").ap()
    build(nc, out=out, **aps)
    got = run_bass_kernel_spmd(nc, [arrays], core_ids=[0])
    return got.results[0]["out"].reshape(B, N, D)
```

```python
from contextlib import ExitStack

import concourse.bass as bass
from concourse import mybir

P = 128
B, N, D = 2, 512, 512
T = B * N
TILES = T // P
TB = N // P
KC = D // P
H0, E0 = 8, 8
HD0 = H0 * E0
H1, E1 = 32, 16
J0 = 1792 // P
J1 = (1376 + P - 1) // P
EARLY = 4
LATE = 5
OT_ON_VECTOR = (4, 5)
EPS = 1e-5
PARTS = 3
ROWS = PARTS * PARTS * E0
STACK = 96
RAW = 2
RING = 8
UNITS = 3 * J0 + 3 * KC + 3 * J1
U_DOWN0, U_QKV1, U_GU1, U_DOWN1 = 2 * J0, 3 * J0, 3 * J0 + 3 * KC, 3 * J0 + 3 * KC + 2 * J1

ALU = mybir.AluOpType
ACT = mybir.ActivationFunctionType
F32, F32R, BF16, I32 = mybir.dt.float32, mybir.dt.float32r, mybir.dt.bfloat16, mybir.dt.int32
AX = mybir.AxisListType


def ring_index(u):
    return u if u < U_QKV1 else u - 3 * KC


def gate_up_order(chunks):
    early = [(j, b) for b in range(B) for j in range(EARLY)]
    return early + [(j, b) for j in range(EARLY, chunks) for b in range(B)]


GU0, GU1 = gate_up_order(J0), gate_up_order(J1)


def build(nc, xT, x, wqkv, bqkv, wo, eye, eye16, units, unit_scale, b1, ffn1_scale, out):
    with ExitStack() as ctx:
        def sb(name, shape, dt=F32, at=ctx):
            return at.enter_context(nc.sbuf_tensor(name, shape, dt))

        def sem(name):
            return ctx.enter_context(nc.semaphore(name))

        banks = [ctx.enter_context(nc.psum_tensor(f"banks{i}", [P, 2, 512], F32)) for i in range(4)]
        bank = [banks[i // 2][:, i % 2, :] for i in range(8)]

        x_tok = sb("x_tok", [P, TILES, D])
        xh = sb("xh", [P, KC, T], F32R)
        xl = sb("xl", [P, KC, T], F32R)
        ring = sb("ring", [P, RING, 2, 512], F32R)
        raw = sb("raw", [P, RAW, 512])
        ident = sb("ident", [P, P])
        ident16 = sb("ident16", [P, P], BF16)
        uscale = sb("uscale", [P, 3 * J0, KC])
        fscale = sb("fscale", [P, 3])
        z = sb("z", [P, 2, D])
        sg = sb("sg", [P, 2, N])
        hf = sb("hf", [P, 2, N])
        stats = sb("stats", [P, 2, 6])
        mv = sb("mv", [P, 2, 2])
        rstd = sb("rstd", [P, 2])
        half = sb("half", [P, 1])
        ones = sb("ones", [P, KC])

        s0 = ExitStack()
        QT = [None, None]
        KT = [None, None]
        Qst = [None, None]
        V0 = [None, None]
        QT[0] = sb("QT0", [P, H0, N], BF16, s0)
        KT[0] = sb("KT0", [P, H0, N], BF16, s0)
        Qst[0] = sb("Qst0", [P, TB, H0, STACK], BF16, s0)
        Kst = sb("Kst", [P, TB, H0, STACK], BF16, s0)
        V0[0] = sb("V00", [P, TB, H0, 32], F32, s0)
        QT[1] = sb("QT1", [P, H0, N], BF16, s0)
        KT[1] = sb("KT1", [P, H0, N], BF16, s0)
        Qst[1] = sb("Qst1", [P, TB, H0, STACK], BF16, s0)
        V0[1] = sb("V01", [P, TB, H0, 32], F32, s0)
        w_qkv = sb("w_qkv", [P, KC, 192], F32, s0)
        b_qkv = sb("b_qkv", [P, 192], F32, s0)
        w_o = sb("w_o", [P, D], F32, s0)
        qkv = sb("qkv", [P, TB, 192], F32, s0)
        smax = sb("smax", [P, TB, H0], F32, s0)
        srest = sb("srest", [P, TB, H0], F32, s0)
        OT = sb("OT", [P, 4, 256], F32, s0)
        o_rec = sb("o_rec", [P, 2, TB, 4], F32, s0)
        o_norm = sb("o_norm", [P, TB, P], F32, s0)
        oT = sb("oT", [P, N], F32, s0)
        with ExitStack() as s0x:
            xT0 = sb("xT0", [P, KC, T], F32, s0x)
            part = sb("part", [P, PARTS, 2, TB, HD0], BF16, s0x)
            rest = sb("rest", [P, 2, TB, HD0], F32, s0x)
        PT = [sb(f"PT{i}", [P, 4, TB, 256], F32, s0) for i in range(2)]
        s0.close()

        with ExitStack() as s1:
            hid0 = sb("hid0", [P, J0, 2, T], F32R, s1)

        with ExitStack() as s2:
            w_qkv1 = sb("w_qkv1", [P, 3, KC, 2, D], F32R, s2)
            bias1 = sb("bias1", [P, 3, D], F32, s2)
            qpad = sb("qpad", [P, H1, 32], F32, s2)
            kpad = sb("kpad", [P, H1, 32], F32, s2)
            qT = sb("qT", [P, 32, H1], F32, s2)
            kT = sb("kT", [P, 32, H1], F32, s2)
            kbd = sb("kbd", [P, 32, 4, H1], F32, s2)
            vs = sb("vs", [P, E1, H1], F32, s2)
            vT = sb("vT", [P, 32, E1], F32, s2)
            vbd = sb("vbd", [P, 32, 4, E1 + 1], F32, s2)
            mx1 = sb("mx1", [P, 32], F32, s2)
            pr = sb("pr", [P, 32, 32], F32, s2)
            prT = sb("prT", [P, 32, 32], F32, s2)
            rec1 = sb("rec1", [P, 32], F32, s2)
            cn = sb("cn", [P, E1, 32], F32, s2)
            ctx1 = sb("ctx1", [P, H1, E1], F32, s2)

        with ExitStack() as s3:
            hid1 = sb("hid1", [P, J1, 2, T], F32R, s3)

        got = {n: sem("got_" + n) for n in
               ("wqkv", "bqkv", "xT0", "xT1", "eye", "x", "wo", "uscale", "fscale", "bias1")}
        raw_in = [sem(f"raw_in{i}") for i in range(RAW)]
        w_ready = sem("w_ready")
        pool_init = sem("pool_init")
        dve_stack, act_stack = sem("dve_stack"), sem("act_stack")
        pool_v = sem("pool_v")
        pool_pads = sem("pool_pads")
        pool_step = sem("pool_step")
        pool_rstd, pool_ve = sem("pool_rstd"), sem("pool_ve")
        pe_qkv0 = sem("pe_qkv0")
        pe_T = sem("pe_T")
        pe_S = sem("pe_S")
        pe_W = sem("pe_W")
        pe_ST = sem("pe_ST")
        pe_PV = sem("pe_PV")
        pe_OT = sem("pe_OT")
        pe_oT = sem("pe_oT")
        pe_y = sem("pe_y")
        pe_xT = sem("pe_xT")
        pe_G = sem("pe_G")
        pe_U = sem("pe_U")
        pe_down = sem("pe_down")
        pe_q1, pe_k1, pe_v1 = sem("pe_q1"), sem("pe_k1"), sem("pe_v1")
        pe_S1, pe_C1 = sem("pe_S1"), sem("pe_C1")
        act_T = sem("act_T")
        act_W = sem("act_W")
        act_exp = sem("act_exp")
        act_oT = sem("act_oT")
        act_xh = sem("act_xh")
        act_silu = sem("act_silu")
        act_hh = sem("act_hh")
        act_kbd, act_vbd, act_E1 = sem("act_kbd"), sem("act_vbd"), sem("act_E1")
        act_ve = sem("act_ve")
        dve_qkv0 = sem("dve_qkv0")
        dve_parts = sem("dve_parts")
        dve_T = sem("dve_T")
        dve_max = sem("dve_max")
        dve_mparts = sem("dve_mparts")
        dve_OT, act_OT = sem("dve_OT"), sem("act_OT")
        dve_on = sem("dve_on")
        dve_z, dve_var = sem("dve_z"), sem("dve_var")
        dve_xn = sem("dve_xn")
        dve_xl = sem("dve_xl")
        dve_h = sem("dve_h")
        dve_hl = sem("dve_hl")
        dve_qe, dve_ke = sem("dve_qe"), sem("dve_ke")
        dve_qT, dve_kT, dve_vT = sem("dve_qT"), sem("dve_kT"), sem("dve_vT")
        dve_sub, dve_prT, dve_cn = sem("dve_sub"), sem("dve_prT"), sem("dve_cn")
        dve_step = sem("dve_step")
        out_done = sem("out_done")

        def unit_used(r):
            layer = r >= U_QKV1
            k = r - layer * U_QKV1
            chunks, order, base = (J0, J1)[layer], (GU0, GU1)[layer], layer * len(GU0)
            if k < 2 * chunks:
                return (pe_G, pe_U)[k % 2], base + order.index((k // 2, B - 1)) + 1
            if k - 2 * chunks < chunks - LATE:
                return pe_down, layer * (J0 - LATE) + k - 2 * chunks + 1
            return pe_y, (2 + layer) * TILES

        def stack_read(n):
            if n >= 8:
                return act_T, 4 + n - 7
            return (act_T, dve_T)[n % 2], n // 2 + 1

        def output_read(u):
            if u in OT_ON_VECTOR:
                return dve_OT, OT_ON_VECTOR.index(u) + 1
            return act_OT, u + 1 - sum(v < u for v in OT_ON_VECTOR)

        def place(rows, a, qk):
            v = rows.rearrange("p t h (i j e) -> p (t h) i j e", i=PARTS, j=PARTS)
            return v[:, :, :, a, :] if qk else v[:, :, a, :, :]

        def spread(a, qk):
            src = part[:, a, qk].rearrange("p t (h e) -> p (t h) e", e=E0)
            return src.unsqueeze(2).to_broadcast([P, TB * H0, PARTS, E0])

        def bank0(t):
            return t % 2 if t < TB else t

        def bank16(i):
            return bank[i].bitcast(BF16)

        block = ctx.enter_context(nc.Block())

        @block.sync
        def _(sp):
            sp.dma_start(w_qkv[:], wqkv).then_inc(got["wqkv"], 16)
            for b in range(B):
                sp.dma_start(xT0[:, :, b * N:(b + 1) * N], xT[b]).then_inc(got[f"xT{b}"], 16)
            sp.dma_start(b_qkv[:], bqkv.partition_broadcast(P)).then_inc(got["bqkv"], 16)
            sp.dma_start(ident[:], eye).then_inc(got["eye"], 16)
            sp.dma_start(ident16[:], eye16).then_inc(got["eye"], 16)
            sp.dma_start(uscale[:], unit_scale.partition_broadcast(P)).then_inc(got["uscale"], 16)
            sp.dma_start(w_o[:], wo).then_inc(got["wo"], 16)
            sp.dma_start(x_tok[:], x.rearrange("(t p) d -> p t d", p=P)).then_inc(got["x"], 16)
            sp.dma_start(fscale[:], ffn1_scale.partition_broadcast(P)).then_inc(got["fscale"], 16)
            for u in range(UNITS):
                if u >= RAW:
                    sp.wait_ge(w_ready, u - RAW + 1)
                sp.dma_start(raw[:, u % RAW, :], units[u]).then_inc(raw_in[u % RAW], 16)
                if u == U_QKV1 + 3 * KC - 1:
                    sp.wait_ge(pe_y, 2 * TILES)
                    sp.dma_start(bias1[:], b1.partition_broadcast(P)).then_inc(got["bias1"], 16)
            for t in range(TILES):
                sp.wait_ge(dve_xn, 3 * TILES + t + 1)
                sp.dma_start(out[t * P:(t + 1) * P, :], x_tok[:, t, :]).then_inc(out_done, 16)
            sp.wait_ge(out_done, 16 * TILES)

        @block.gpsimd
        def _(pool):
            ms = nc.gpsimd.memset
            steps = [0]

            def step(ins):
                steps[0] += 1
                ins.then_inc(pool_step, 1)
                pool.wait_ge(pool_step, steps[0])

            def inverse_deviation(n):
                pool.wait_ge(dve_var, n + 1)
                if n >= 2:
                    pool.wait_ge(dve_xn, n - 1)
                nc.gpsimd.tensor_tensor(rstd[:, n % 2:n % 2 + 1], mv[:, n % 2, 1:2], half[:], ALU.pow)\
                    .then_inc(pool_rstd, 1)

            ms(ones[:], 1.0)
            ms(half[:], -0.5)
            ms(Kst[:, :, :, ROWS:ROWS + 3], 1.0)
            ms(Kst[:, :, :, ROWS + 3:STACK], 0.0)
            for b in range(B):
                ms(Qst[b][:, :, :, ROWS:STACK], 0.0)
                ms(V0[b][:, :, :, E0:E0 + 1], 1.0)
                ms(V0[b][:, :, :, E0 + 1:], 0.0)
            ms(o_norm[:, :, HD0:HD0 + 1], 1.0)
            step(ms(o_norm[:, :, HD0 + 1:], 0.0))
            for a in (QT[0], KT[0], QT[1]):
                step(ms(a[STACK:P, :, :].bitcast(F32), 0.0))
            ms(KT[1][STACK:P, :, :].bitcast(F32), 0.0).then_inc(pool_init, 1)
            pool.wait_ge(pool_init, 1)
            for b in range(B):
                pool.wait_ge(dve_parts, b + 1)
                nc.gpsimd.tensor_copy(V0[b][:, :, :, 0:E0],
                                      qkv[:, :, 2 * HD0:].rearrange("p t (h e) -> p t h e", e=E0)).then_inc(pool_v, 1)

            pool.wait_ge(got["uscale"], 16)
            for u in range(UNITS):
                if u == RING:
                    for n in range(TILES):
                        inverse_deviation(n)
                if U_GU1 - TILES < u < U_GU1:
                    inverse_deviation(2 * TILES - 1 - U_GU1 + u)
                if u == U_GU1:
                    pool.wait_ge(pe_y, 2 * TILES)
                    ms(qpad[:, :, E1:], 0.0)
                    ms(kpad[:, :, E1:], 0.0).then_inc(pool_pads, 1)
                    inverse_deviation(2 * TILES - 1)
                    ms(kbd[:], 0.0)
                    ms(vbd[:, :, :, 0:E1], 0.0)
                    step(ms(vbd[:, :, :, E1:], 0.0))
                    for g in range(3):
                        step(ms(vbd[32 * g:32 * g + 32, :, g, E1:], 1.0))
                    ms(vbd[96:P, :, 3, E1:], 1.0).then_inc(pool_pads, 1)
                    pool.wait_ge(pool_pads, 2)
                    pool.wait_ge(got["bias1"], 16)
                if U_GU1 <= u < U_GU1 + TILES:
                    s = u - U_GU1
                    if s >= 2:
                        inverse_deviation(2 * TILES + s - 2)
                    pool.wait_ge(act_ve, s + 1)
                    v = vs[:].rearrange("p e h -> p h e")
                    nc.gpsimd.tensor_tensor(v, v, bias1[:, 2, :].rearrange("p (h e) -> p h e", e=E1),
                                            ALU.add).then_inc(pool_ve, 1)
                if u == U_GU1 + TILES:
                    for n in range(3 * TILES - 2, 3 * TILES):
                        inverse_deviation(n)
                w = raw[:, u % RAW, :]
                if U_QKV1 <= u < U_GU1:
                    k = u - U_QKV1
                    dst = w_qkv1[:, k // KC, k % KC]
                    if k % 2 == 0:
                        pool.wait_ge(pe_down, k // 2 + 1)
                else:
                    r = ring_index(u)
                    dst = ring[:, r % RING]
                    if r >= RING:
                        pool.wait_ge(*unit_used(r - RING))
                pool.wait_ge(raw_in[u % RAW], 16 * (u // RAW + 1))
                scale = uscale[:, u, :] if u < U_QKV1 else ones[:]
                by = scale.unsqueeze(2).to_broadcast([P, KC, P])
                w, hi, lo = (a.rearrange("p (c m) -> p c m", c=KC) for a in (w, dst[:, 0, :], dst[:, 1, :]))
                ins = nc.gpsimd.tensor_tensor(hi, w, by, ALU.mult)
                if u < U_QKV1:
                    ins = nc.gpsimd.tensor_tensor(w, w, by, ALU.mult)
                step(ins)
                nc.gpsimd.tensor_tensor(lo, w, hi.bitcast(F32), ALU.subtract).then_inc(w_ready, 1)
            for n in range(3 * TILES, 4 * TILES):
                inverse_deviation(n)

        @block.tensor
        def _(pe):
            def split_product(psum, sh, sl, mh, ml, first, last):
                nc.tensor.matmul(psum, sh, mh, start=first, stop=False)
                nc.tensor.matmul(psum, sh, ml, start=False, stop=False)
                return nc.tensor.matmul(psum, sl, mh, start=False, stop=last)

            def project0(t):
                if t == 0:
                    pe.wait_ge(got["wqkv"], 16)
                if t % TB == 0:
                    pe.wait_ge(got[f"xT{t // TB}"], 16)
                if t >= 2:
                    pe.wait_ge(dve_qkv0, t - 1)
                for c in range(KC):
                    mm = nc.tensor.matmul(bank[t % 2][:, 0:192], xT0[:, c, t * P:(t + 1) * P], w_qkv[:, c, :],
                                          start=(c == 0), stop=(c == KC - 1))
                mm.then_inc(pe_qkv0, 1)

            def transpose_stack(b, fills):
                if b == 0:
                    pe.wait_ge(got["eye"], 32)
                for i in fills:
                    n = 8 * b + i
                    pe.wait_ge(dve_stack if i < 4 else act_stack, b + 1)
                    if n >= 6:
                        pe.wait_ge(*stack_read(n - 6))
                    src = Kst if i < 4 else Qst[b]
                    for hh in range(2):
                        for t in range(TB):
                            c = hh * N + t * P
                            mm = nc.tensor.transpose(bank16(2 + n % 6)[0:STACK, c:c + P],
                                                     src[:, t, 2 * (i % 4) + hh, :], ident16[:])
                    mm.then_inc(pe_T, 1)

            def scores_for_max(b, tiles):
                for i in tiles:
                    h, t = divmod(i, TB)
                    n = b * H0 * TB + i
                    if n == 0:
                        pe.wait_ge(pool_init, 1)
                    if i == 0:
                        pe.wait_ge(act_T, (4, 12)[b])
                        pe.wait_ge(dve_T, 4)
                    if n >= 2:
                        pe.wait_ge(dve_max, n - 1)
                    nc.tensor.matmul(bank[n % 2], QT[b][:, h, t * P:(t + 1) * P], KT[b][:, h, :],
                                     start=True, stop=True).then_inc(pe_S, 1)

            def transpose_max(b):
                pe.wait_ge(dve_mparts, b + 1)
                if b == 0:
                    pe.wait_ge(act_T, 12)
                for i in range(4):
                    n = 4 * b + i
                    if i >= 2:
                        pe.wait_ge(act_W, n - 1)
                    for hh in range(2):
                        for t in range(TB):
                            c = hh * N + t * P
                            mm = nc.tensor.transpose(bank16((6, 0)[b] + n % 2)[64:STACK, c:c + P],
                                                     Qst[b][:, t, 2 * i + hh, 64:STACK], ident16[:])
                    mm.then_inc(pe_W, 1)

            def scores_transposed(u, i):
                b, g, half = u // 4, u // 2 % 2, u % 2
                n = 4 * u + i
                if n % 16 == 0:
                    pe.wait_ge(act_W, 4 * b + 4)
                if n >= 2:
                    pe.wait_ge(act_exp, n - 1)
                for kt in range(TB):
                    mm = nc.tensor.matmul(
                        banks[1 + n % 2][:, kt // 2, (kt % 2) * 256:(kt % 2) * 256 + 256],
                        KT[b][:, 4 * g + i, kt * P:(kt + 1) * P],
                        QT[b][:, 4 * g + i, half * 256:(half + 1) * 256], start=True, stop=True)
                mm.then_inc(pe_ST, 1)

            def weigh_values(u, kt):
                b, g = u // 4, u // 2 % 2
                if kt == 0:
                    pe.wait_ge(act_exp, 4 * u + 4)
                    pe.wait_ge(pool_v, b + 1)
                    if u >= 2:
                        pe.wait_ge(*output_read(u - 2))
                for i in range(4):
                    mm = nc.tensor.matmul(bank[6 + u % 2][32 * i:32 * i + 32, 0:256],
                                          V0[b][:, kt, 4 * g + i, :], PT[u % 2][:, i, kt, :],
                                          start=(kt == 0), stop=(kt == TB - 1), skip_group_check=True)
                if kt == TB - 1:
                    mm.then_inc(pe_PV, 1)

            def output_to_tokens(b):
                if b == 0:
                    pe.wait_ge(act_W, 8)
                else:
                    pe.wait_ge(act_exp, 32)
                for u in range(4 * b, 4 * b + 4):
                    pe.wait_ge(*output_read(u))
                for g in range(2):
                    for t in range(TB):
                        mm = nc.tensor.transpose(bank[(0, 4)[b] + g][:, t * P:(t + 1) * P],
                                                 OT[:, 2 * g + t // 2, (t % 2) * P:(t % 2) * P + P], ident[:])
                    mm.then_inc(pe_OT, 1)

            def output_to_features(b):
                pe.wait_ge(dve_on, 2 * b + 2)
                pe.wait_ge(pool_init, 1)
                for t in range(TB):
                    mm = nc.tensor.transpose(bank[(0, 4)[b]][:, t * P:(t + 1) * P], o_norm[:, t, :], ident[:])
                mm.then_inc(pe_oT, 1)

            def output_product(t):
                if t % TB == 0:
                    pe.wait_ge(act_oT, t // TB + 1)
                if t == 0:
                    pe.wait_ge(got["wo"], 16)
                if t in (2, 3):
                    pe.wait_ge(dve_xl, t - 1)
                c = (t % TB) * P
                nc.tensor.matmul(bank[bank0(t)], oT[:, c:c + P], w_o[:], start=True, stop=True).then_inc(pe_y, 1)

            def transpose_x(layer, t, to):
                n = layer * TILES + t
                pe.wait_ge(dve_xn, n + 1)
                if layer == 2 and t > 0:
                    pe.wait_ge(dve_xl, n)
                for c in range(KC):
                    mm = nc.tensor.transpose(bank[to][:, c * P:(c + 1) * P], x_tok[:, t, c * P:(c + 1) * P], ident[:])
                mm.then_inc(pe_xT, 1)

            def gate_up(layer, k):
                j, b = (GU0, GU1)[layer][k]
                kk = k + layer * len(GU0)
                u = (0, U_GU1)[layer] + 2 * j
                if j == 0:
                    ready = (0, 2 * TILES)[layer] + TB * (b + 1)
                    pe.wait_ge(dve_xl, ready)
                if k == 0 and layer == 0:
                    pe.wait_ge(act_exp, 4 * 8)
                if k == 0 and layer == 1:
                    pe.wait_ge(dve_ke, TILES)
                for what, psum, done, free in ((0, bank[(2, 0)[layer]], pe_G, act_silu),
                                               (1, bank[(3, 1)[layer]], pe_U, dve_h)):
                    pe.wait_ge(w_ready, u + what + 1)
                    if kk >= 1:
                        pe.wait_ge(free, kk)
                    w = ring[:, ring_index(u + what) % RING].rearrange("p s (c m) -> p s c m", c=KC)
                    cols = slice(b * N, (b + 1) * N)
                    for c in range(KC):
                        mm = split_product(psum, w[:, 0, c, :], w[:, 1, c, :], xh[:, c, cols], xl[:, c, cols],
                                           c == 0, c == KC - 1)
                    mm.then_inc(done, 1)

            def down_chunk(layer, j, t):
                chunks = (J0, J1)[layer]
                hid = (hid0, hid1)[layer]
                w = ring[:, ring_index((U_DOWN0, U_DOWN1)[layer] + j) % RING]
                cols = slice(t * P, (t + 1) * P)
                return split_product(bank[t], hid[:, j, 0, cols], hid[:, j, 1, cols], w[:, 0, :], w[:, 1, :],
                                     j == 0, j == chunks - 1)

            def down(layer, between):
                chunks = (J0, J1)[layer]
                base = layer * len(GU0)
                order = ([6, 7, 0, 1, 4, 5, 2, 3], [2, 3, 4, 5, 6, 7, 0, 1])[layer]
                for j in range(chunks - LATE):
                    pe.wait_ge(w_ready, (U_DOWN0, U_DOWN1)[layer] + j + 1)
                    pe.wait_ge(dve_hl, base + max(k for k, x in enumerate((GU0, GU1)[layer]) if x[0] == j) + 1)
                    for t in order:
                        if j == 0 and t == order[-2]:
                            pe.wait_ge(act_silu, base + 2 * chunks)
                        if j == 0 and t == order[-1]:
                            pe.wait_ge(dve_h, base + 2 * chunks)
                        mm = down_chunk(layer, j, t)
                    mm.then_inc(pe_down, 1)
                pe.wait_ge(dve_hl, base + 2 * chunks)
                pe.wait_ge(w_ready, (U_DOWN0, U_DOWN1)[layer] + chunks)
                for t in range(TILES):
                    for j in range(chunks - LATE, chunks):
                        mm = down_chunk(layer, j, t)
                    mm.then_inc(pe_y, 1)
                    between(t)

            def project1(t):
                cols = slice(t * P, (t + 1) * P)
                if t == 0:
                    pe.wait_ge(w_ready, U_GU1)
                pe.wait_ge(dve_xl, TILES + t + 1)
                if t == 0:
                    pe.wait_ge(dve_xl, TILES + 3)
                for i, (done, free) in enumerate(((pe_q1, dve_qe), (pe_k1, dve_ke), (pe_v1, act_ve))):
                    if t:
                        pe.wait_ge(free, t)
                    for c in range(KC):
                        sh, sl = xh[:, c, cols], xl[:, c, cols]
                        mm = split_product(bank[i], sh, sl, w_qkv1[:, i, c, 0, :], w_qkv1[:, i, c, 1, :],
                                           c == 0, c == KC - 1)
                    mm.then_inc(done, 1)

            def scores1(t):
                pe.wait_ge(dve_qT, t + 1)
                pe.wait_ge(act_kbd, t + 1)
                if t == 0:
                    pe.wait_ge(dve_xl, TILES + 6)
                if t:
                    pe.wait_ge(dve_sub, t)
                for s in range(8):
                    for j in range(4):
                        i = 4 * s + j
                        mm = nc.tensor.matmul(bank[4 + s // 4][32 * j:32 * j + 32, (s % 4) * P:(s % 4 + 1) * P],
                                              qT[:, i, :], kbd[:, i, :, :], start=True, stop=True,
                                              skip_group_check=True)
                mm.then_inc(pe_S1, 1)

            def context1(t):
                pe.wait_ge(dve_prT, t + 1)
                pe.wait_ge(act_vbd, t + 1)
                if t == 0:
                    pe.wait_ge(dve_xl, 2 * TILES)
                    pe.wait_ge(pool_pads, 2)
                if t:
                    pe.wait_ge(dve_cn, t)
                W = 4 * (E1 + 1)
                for s in range(8):
                    for g in range(4):
                        mm = nc.tensor.matmul(bank[6 + s // 4][32 * g:32 * g + 32, (s % 4) * W:(s % 4 + 1) * W],
                                              prT[:, 4 * s + g, :], vbd[:, 4 * s + g, :, :], start=True, stop=True,
                                              skip_group_check=True)
                mm.then_inc(pe_C1, 1)

            for t in range(TILES):
                project0(t)
            transpose_stack(0, range(8))
            for h in range(H0):
                scores_for_max(0, range(4 * h, 4 * h + 4))
                if 3 <= h < 7:
                    transpose_stack(1, range(2 * h - 6, 2 * h - 4))
            scores_for_max(1, range(4))
            transpose_max(0)
            for u in range(4):
                for i in range(4):
                    scores_transposed(u, i)
                    n = 4 + 2 * (4 * u + i)
                    scores_for_max(1, range(n, min(n + 2, 32)))
                    if u:
                        weigh_values(u - 1, i)
            for kt in range(TB):
                weigh_values(3, kt)
            transpose_max(1)
            output_to_tokens(0)
            for u in range(4, 8):
                for i in range(4):
                    scores_transposed(u, i)
                    if u > 4:
                        weigh_values(u - 1, i)
                    if (u, i) == (4, 1):
                        output_to_features(0)
                    if (u, i) == (4, 2):
                        output_product(0)
                        output_product(1)
                    if (u, i) == (6, 1):
                        transpose_x(0, 0, 0)
                        transpose_x(0, 1, 1)
                    if (u, i) == (6, 3):
                        output_product(2)
                        output_product(3)
            for kt in range(TB):
                weigh_values(7, kt)
            output_to_tokens(1)
            transpose_x(0, 2, 0)
            transpose_x(0, 3, 1)
            output_to_features(1)
            for t in range(TB, TILES):
                output_product(t)
            gate_up(0, 0)
            gate_up(0, 1)
            transpose_x(0, 4, 4)
            transpose_x(0, 5, 5)
            gate_up(0, 2)
            transpose_x(0, 6, 6)
            transpose_x(0, 7, 7)
            for k in range(3, len(GU0)):
                gate_up(0, k)

            def after_down0(t):
                if t >= 3 and t % 2 == 1:
                    transpose_x(1, t - 3, t - 3)
                    transpose_x(1, t - 2, t - 2)

            down(0, after_down0)
            for s in range(TILES):
                project1(s)
                if s == 0:
                    transpose_x(1, 6, 6)
                    transpose_x(1, 7, 7)
                late = s >= 4 and s % 2 == 0
                if late:
                    transpose_x(2, s - 4, 3)
                if s >= 1:
                    scores1(s - 1)
                if late:
                    transpose_x(2, s - 3, 3)
                if s >= 2:
                    context1(s - 2)
            gate_up(1, 0)
            transpose_x(2, 4, 3)
            scores1(7)
            transpose_x(2, 5, 3)
            context1(6)
            gate_up(1, 1)
            context1(7)
            gate_up(1, 2)
            transpose_x(2, 6, 3)
            transpose_x(2, 7, 3)
            for k in range(3, len(GU1)):
                gate_up(1, k)
            down(1, lambda t: None)

        @block.scalar
        def _(act):
            def stack_q(b):
                act.wait_ge(dve_parts, b + 1)
                if b == 0:
                    act.wait_ge(pool_init, 1)
                for a in range(PARTS):
                    ins = nc.scalar.copy(place(Qst[b][:, :, :, 0:ROWS], a, 0), spread(a, 0))
                ins.then_inc(act_stack, 1)

            def evacuate_stack(n):
                act.wait_ge(pe_T, n + 1)
                b, i = divmod(n, 8)
                dst = (KT if i < 4 else QT)[b][0:STACK, 2 * (i % 4):2 * (i % 4) + 2, :]
                nc.scalar.copy(dst, bank16(2 + n % 6)[0:STACK, :].rearrange("p (h n) -> p h n", h=2)).then_inc(act_T, 1)

            def evacuate_max(b):
                for n in range(4 * b, 4 * b + 4):
                    act.wait_ge(pe_W, n + 1)
                    i = n % 4
                    nc.scalar.copy(QT[b][64:STACK, 2 * i:2 * i + 2, :],
                                   bank16((6, 0)[b] + n % 2)[64:STACK, :].rearrange("p (h n) -> p h n", h=2))\
                        .then_inc(act_W, 1)

            def exponential(u, i):
                if u >= 2 and i == 0:
                    act.wait_ge(pe_PV, u - 1)
                n = 4 * u + i
                act.wait_ge(pe_ST, n + 1)
                nc.scalar.activation(PT[u % 2][:, i].rearrange("p k n -> p (k n)"),
                                     banks[1 + n % 2][:].rearrange("p k n -> p (k n)"), ACT.Exp).then_inc(act_exp, 1)

            def evacuate_output(u):
                act.wait_ge(pe_PV, u + 1)
                if u >= 4:
                    act.wait_ge(pe_OT, 2)
                nc.scalar.copy(OT[:, u % 4, :], bank[6 + u % 2][:, 0:256]).then_inc(act_OT, 1)

            def evacuate_oT(b):
                act.wait_ge(pe_oT, b + 1)
                nc.scalar.copy(oT[:], bank[(0, 4)[b]]).then_inc(act_oT, 1)

            def x_hi(n, bk):
                act.wait_ge(pe_xT, n + 1)
                t = n % TILES
                nc.scalar.copy(xh[:, :, t * P:(t + 1) * P],
                               bank[bk].rearrange("p (c n) -> p c n", c=KC)).then_inc(act_xh, 1)

            def hidden(layer, k):
                kk = k + layer * len(GU0)
                j, b = (GU0, GU1)[layer][k]
                act.wait_ge(pe_G, kk + 1)
                if kk >= 2:
                    act.wait_ge(dve_h, kk - 1)
                if layer and k == 0:
                    act.wait_ge(got["fscale"], 16)
                nc.scalar.activation(sg[:, kk % 2, :], bank[(2, 0)[layer]], ACT.Silu,
                                     scale=fscale[:, 0:1] if layer else 1.0).then_inc(act_silu, 1)
                act.wait_ge(dve_h, kk + 1)
                nc.scalar.copy((hid0, hid1)[layer][:, j, 0, b * N:(b + 1) * N], hf[:, kk % 2, :]).then_inc(act_hh, 1)

            stack_q(0)
            for n in range(0, 8, 2):
                evacuate_stack(n)
            stack_q(1)
            for n in range(8, 16):
                evacuate_stack(n)
            evacuate_max(0)
            for u in range(4):
                for i in range(4):
                    exponential(u, i)
                if u:
                    evacuate_output(u - 1)
            evacuate_output(3)
            evacuate_max(1)
            for u in range(4, 8):
                for i in range(4):
                    exponential(u, i)
                    if (u, i) == (4, 1):
                        evacuate_oT(0)
                    if (u, i) == (6, 1):
                        x_hi(0, 0)
                        x_hi(1, 1)
            evacuate_output(6)
            evacuate_output(7)
            x_hi(2, 0)
            x_hi(3, 1)
            evacuate_oT(1)
            hidden(0, 0)
            hidden(0, 1)
            x_hi(4, 4)
            x_hi(5, 5)
            hidden(0, 2)
            x_hi(6, 6)
            x_hi(7, 7)
            for k in range(3, len(GU0)):
                hidden(0, k)
            for t in range(TILES):
                x_hi(TILES + t, t)

            def k_blocks(t):
                act.wait_ge(dve_kT, t + 1)
                if t == 0:
                    act.wait_ge(pool_pads, 2)
                else:
                    act.wait_ge(pe_S1, t)
                for g in range(4):
                    rows = slice(32 * g, 32 * g + 32)
                    ins = nc.scalar.copy(kbd[rows, :, g, :], kT[rows])
                ins.then_inc(act_kbd, 1)

            def v_blocks(t):
                act.wait_ge(dve_vT, t + 1)
                if t == 0:
                    act.wait_ge(pool_pads, 2)
                else:
                    act.wait_ge(pe_C1, t)
                for j in range(4):
                    to = vbd[32 * j:32 * j + 32].rearrange("p (s g) i e -> p s g i e", g=4)
                    for g in range(4):
                        ins = nc.scalar.copy(to[:, :, g, j, 0:E1],
                                             vT[32 * g:32 * g + 32].rearrange("p (s i) e -> p s i e", i=4)[:, :, j, :])
                ins.then_inc(act_vbd, 1)

            def evacuate_v(t):
                act.wait_ge(pe_v1, t + 1)
                if t == 0:
                    act.wait_ge(pe_y, 2 * TILES)
                else:
                    act.wait_ge(dve_vT, t)
                nc.scalar.copy(vs[:].rearrange("p e h -> p h e"),
                               bank[2].rearrange("p (h e) -> p h e", e=E1)).then_inc(act_ve, 1)

            def exp1(t):
                act.wait_ge(dve_sub, t + 1)
                nc.scalar.activation(pr[:], pr[:], ACT.Exp, scale=E1 ** -0.5).then_inc(act_E1, 1)

            for s in range(TILES):
                late = s >= 4 and s % 2 == 0
                if late:
                    x_hi(2 * TILES + s - 4, 3)
                if s >= 1:
                    exp1(s - 1)
                if late:
                    x_hi(2 * TILES + s - 3, 3)
                if s >= 1:
                    v_blocks(s - 1)
                evacuate_v(s)
                k_blocks(s)
            hidden(1, 0)
            x_hi(2 * TILES + 4, 3)
            exp1(7)
            x_hi(2 * TILES + 5, 3)
            v_blocks(7)
            hidden(1, 1)
            hidden(1, 2)
            x_hi(2 * TILES + 6, 3)
            x_hi(2 * TILES + 7, 3)
            for k in range(3, len(GU1)):
                hidden(1, k)

        @block.vector
        def _(dve):
            tt, ts = nc.vector.tensor_tensor, nc.vector.tensor_scalar
            steps = [0]

            def step(ins):
                steps[0] += 1
                ins.then_inc(dve_step, 1)
                dve.wait_ge(dve_step, steps[0])

            def evacuate_qkv(t):
                if t == 0:
                    dve.wait_ge(got["bqkv"], 16)
                if t == TB:
                    dve.wait_ge(pool_v, 1)
                dve.wait_ge(pe_qkv0, t + 1)
                tt(qkv[:, t % TB, :], bank[t % 2][:, 0:192], b_qkv[:], ALU.add).then_inc(dve_qkv0, 1)

            def split_qk(b):
                dve.wait_ge(dve_qkv0, TB * (b + 1))
                if b:
                    dve.wait_ge(dve_parts, 1)
                    dve.wait_ge(dve_stack, 1)
                    dve.wait_ge(act_stack, 1)
                qk = qkv[:, :, 0:2 * HD0].rearrange("p t (q x) -> p q t x", q=2)
                step(nc.vector.tensor_copy(part[:, 0], qk))
                step(tt(rest[:], qk, part[:, 0], ALU.subtract))
                step(nc.vector.tensor_copy(part[:, 1], rest[:]))
                step(tt(rest[:], rest[:], part[:, 1], ALU.subtract))
                nc.vector.tensor_copy(part[:, 2], rest[:]).then_inc(dve_parts, 1)

            def stack_k(b):
                dve.wait_ge(dve_parts, b + 1)
                if b == 0:
                    dve.wait_ge(pool_init, 1)
                else:
                    dve.wait_ge(pe_T, 4)
                for a in range(PARTS):
                    ins = nc.vector.tensor_copy(place(Kst[:, :, :, 0:ROWS], a, 1), spread(a, 1))
                ins.then_inc(dve_stack, 1)

            def evacuate_stack(n):
                dve.wait_ge(pe_T, n + 1)
                b, i = divmod(n, 8)
                dst = (KT if i < 4 else QT)[b][0:STACK, 2 * (i % 4):2 * (i % 4) + 2, :]
                nc.vector.tensor_copy(dst, bank16(2 + n % 6)[0:STACK, :].rearrange("p (h n) -> p h n", h=2)).then_inc(dve_T, 1)

            def maxima(b, h):
                if b == 1 and h == 0:
                    dve.wait_ge(dve_mparts, 1)
                for t in range(TB):
                    n = (b * H0 + h) * TB + t
                    dve.wait_ge(pe_S, n + 1)
                    nc.vector.tensor_reduce(smax[:, t, h:h + 1], bank[n % 2], AX.X, ALU.max,
                                            negate=True).then_inc(dve_max, 1)

            def split_max(b):
                dve.wait_ge(dve_max, 32 * (b + 1))
                if b:
                    dve.wait_ge(dve_mparts, 1)
                if b == 0:
                    dve.wait_ge(pool_init, 1)
                to = [Qst[b][:, :, :, ROWS + a] for a in range(PARTS)]
                step(nc.vector.tensor_copy(to[0], smax[:]))
                step(tt(srest[:], smax[:], to[0], ALU.subtract))
                step(nc.vector.tensor_copy(to[1], srest[:]))
                step(tt(srest[:], srest[:], to[1], ALU.subtract))
                nc.vector.tensor_copy(to[2], srest[:]).then_inc(dve_mparts, 1)

            def evacuate_output(u):
                dve.wait_ge(pe_PV, u + 1)
                dve.wait_ge(pe_OT, 2)
                nc.vector.tensor_copy(OT[:, u % 4, :], bank[6 + u % 2][:, 0:256]).then_inc(dve_OT, 1)

            def normalise_output(b):
                if b == 0:
                    dve.wait_ge(pool_init, 1)
                else:
                    dve.wait_ge(dve_on, 2)
                    dve.wait_ge(pe_oT, 1)
                for g in range(2):
                    dve.wait_ge(pe_OT, 2 * b + g + 1)
                    o = bank[(0, 4)[b] + g].rearrange("p (t h e) -> p t h e", t=TB, h=4)
                    step(nc.vector.reciprocal(o_rec[:, g], o[:, :, :, E0]))
                    nc.vector.scalar_tensor_tensor(
                        out=o_norm[:, :, g * 32:(g + 1) * 32].rearrange("p t (h e) -> p t h e", h=4),
                        in0=o[:, :, :, 0:E0], scalar=HD0 ** -0.5,
                        in1=o_rec[:, g].unsqueeze(3).to_broadcast([P, TB, 4, E0]),
                        op0=ALU.mult, op1=ALU.mult).then_inc(dve_on, 1)

            def x_lo(n, bk):
                dve.wait_ge(act_xh, n + 1)
                t = n % TILES
                tt(xl[:, :, t * P:(t + 1) * P], bank[bk].rearrange("p (c n) -> p c n", c=KC),
                   xh[:, :, t * P:(t + 1) * P].bitcast(F32), ALU.subtract).then_inc(dve_xl, 1)

            def add_residual(n, src):
                layer, t = divmod(n, TILES)
                zz = z[:, n % 2, :]
                if layer != 2:
                    dve.wait_ge(pe_y, n + 1 - (TILES if layer == 3 else 0))
                if n == 0:
                    dve.wait_ge(got["x"], 16)
                elif n >= 2:
                    dve.wait_ge(dve_xn, n - 1)
                if layer == 3:
                    ins = nc.vector.scalar_tensor_tensor(out=zz, in0=src, scalar=fscale[:, 2:3], in1=x_tok[:, t, :],
                                                         op0=ALU.mult, op1=ALU.add)
                else:
                    ins = tt(zz, src, x_tok[:, t, :], ALU.add)
                ins.then_inc(dve_z, 1)
                dve.wait_ge(dve_z, n + 1)
                step(nc.vector.bn_stats(stats[:, n % 2, :], zz))
                if n >= 2:
                    dve.wait_ge(pool_rstd, n - 1)
                step(nc.vector.bn_aggr(mv[:, n % 2, :], stats[:, n % 2, :]))
                ts(mv[:, n % 2, 1:2], mv[:, n % 2, 1:2], EPS, None, ALU.add).then_inc(dve_var, 1)

            def normalise(n):
                dve.wait_ge(dve_var, n + 1)
                dve.wait_ge(pool_rstd, n + 1)
                ts(x_tok[:, n % TILES, :], z[:, n % 2, :], mv[:, n % 2, 0:1], rstd[:, n % 2:n % 2 + 1],
                   ALU.subtract, ALU.mult).then_inc(dve_xn, 1)

            def layernorm_pair(n, banks_):
                add_residual(n, bank[banks_[0]])
                add_residual(n + 1, bank[banks_[1]])
                normalise(n)
                normalise(n + 1)

            def hidden(layer, k):
                kk = k + layer * len(GU0)
                j, b = (GU0, GU1)[layer][k]
                dve.wait_ge(act_silu, kk + 1)
                dve.wait_ge(pe_U, kk + 1)
                if kk >= 2:
                    dve.wait_ge(dve_hl, kk - 1)
                h = hf[:, kk % 2, :]
                if layer == 0:
                    tt(h, bank[3], sg[:, kk % 2, :], ALU.mult).then_inc(dve_h, 1)
                else:
                    if k == 0:
                        dve.wait_ge(got["fscale"], 16)
                    nc.vector.scalar_tensor_tensor(out=h, in0=bank[1], scalar=fscale[:, 1:2], in1=sg[:, kk % 2, :],
                                                   op0=ALU.mult, op1=ALU.mult).then_inc(dve_h, 1)
                dve.wait_ge(act_hh, kk + 1)
                hid = (hid0, hid1)[layer]
                tt(hid[:, j, 1, b * N:(b + 1) * N], h, hid[:, j, 0, b * N:(b + 1) * N].bitcast(F32),
                   ALU.subtract).then_inc(dve_hl, 1)

            for t in range(TB):
                evacuate_qkv(t)
            split_qk(0)
            stack_k(0)
            for t in range(TB, TILES):
                evacuate_qkv(t)
            for n in range(1, 8, 2):
                evacuate_stack(n)
            maxima(0, 0)
            split_qk(1)
            stack_k(1)
            for h in range(1, H0):
                maxima(0, h)
            split_max(0)
            for h in range(H0):
                maxima(1, h)
            split_max(1)
            normalise_output(0)
            layernorm_pair(0, (0, 1))
            evacuate_output(4)
            x_lo(0, 0)
            x_lo(1, 1)
            evacuate_output(5)
            layernorm_pair(2, (0, 1))
            normalise_output(1)
            x_lo(2, 0)
            x_lo(3, 1)
            layernorm_pair(4, (4, 5))
            hidden(0, 0)
            layernorm_pair(6, (6, 7))
            hidden(0, 1)
            x_lo(4, 4)
            x_lo(5, 5)
            hidden(0, 2)
            x_lo(6, 6)
            x_lo(7, 7)
            for k in range(3, len(GU0)):
                hidden(0, k)
            for t in range(0, TILES, 2):
                layernorm_pair(TILES + t, (t, t + 1))
                if t >= 2:
                    x_lo(TILES + t - 2, t - 2)
                    x_lo(TILES + t - 1, t - 1)

            def evacuate1(t):
                if t == 0:
                    dve.wait_ge(got["bias1"], 16)
                    dve.wait_ge(pool_pads, 1)
                else:
                    dve.wait_ge(dve_kT, t)
                for i, (seen, done) in enumerate(((pe_q1, dve_qe), (pe_k1, dve_ke))):
                    dve.wait_ge(seen, t + 1)
                    to = (qpad, kpad)[i][:, :, 0:E1]
                    tt(to, bank[i].rearrange("p (h e) -> p h e", e=E1),
                       bias1[:, i, :].rearrange("p (h e) -> p h e", e=E1), ALU.add).then_inc(done, 1)

            def turn_qk(t):
                dve.wait_ge(dve_ke, t + 1)
                if t:
                    dve.wait_ge(pe_S1, t)
                nc.vector.transpose(qT[:].rearrange("p i h -> p h i"), qpad[:]).then_inc(dve_qT, 1)
                if t:
                    dve.wait_ge(act_kbd, t)
                nc.vector.transpose(kT[:].rearrange("p i h -> p h i"), kpad[:]).then_inc(dve_kT, 1)

            def turn_v(t):
                dve.wait_ge(pool_ve, t + 1)
                if t:
                    dve.wait_ge(act_vbd, t)
                nc.vector.transpose(vT[:].rearrange("p i e -> p e i"), vs[:]).then_inc(dve_vT, 1)

            def softmax1(t):
                dve.wait_ge(pe_S1, t + 1)
                if t:
                    dve.wait_ge(dve_sub, t)
                    dve.wait_ge(dve_prT, t)
                s = banks[2][:].rearrange("p b (i h) -> p (b i) h", h=H1)
                step(nc.vector.tensor_reduce(mx1[:], s, AX.X, ALU.max))
                tt(pr[:], s, mx1[:].unsqueeze(2).to_broadcast([P, 32, H1]), ALU.subtract).then_inc(dve_sub, 1)

            def turn_probs(t):
                dve.wait_ge(act_E1, t + 1)
                if t:
                    dve.wait_ge(pe_C1, t)
                nc.vector.transpose(prT[:], pr[:]).then_inc(dve_prT, 1)

            def context_norm(t):
                dve.wait_ge(pe_C1, t + 1)
                if t:
                    dve.wait_ge(dve_cn, t)
                c = banks[3][:, :, 0:16 * (E1 + 1)].rearrange("p b (i e) -> p b i e", e=E1 + 1)
                rec = rec1[:].rearrange("p (b i) -> p b i", b=2)
                step(nc.vector.reciprocal(rec, c[:, :, :, E1]))
                for i in range(2):
                    ins = tt(cn[:, :, 16 * i:16 * i + 16].rearrange("p e i -> p i e"), c[:, i, :, 0:E1],
                             rec1[:, 16 * i:16 * i + 16].unsqueeze(2).to_broadcast([P, 16, E1]), ALU.mult)
                ins.then_inc(dve_cn, 1)
                dve.wait_ge(dve_cn, t + 1)
                step(nc.vector.transpose(ctx1[:].rearrange("p h e -> p e h"), cn[:]))
                add_residual(2 * TILES + t, ctx1[:].rearrange("p h e -> p (h e)"))
                normalise(2 * TILES + t)

            for s in range(TILES):
                late = s >= 4 and s % 2 == 0
                evacuate1(s)
                if s == 0:
                    x_lo(TILES + 6, 6)
                    x_lo(TILES + 7, 7)
                if late:
                    x_lo(2 * TILES + s - 4, 3)
                if s >= 1:
                    softmax1(s - 1)
                turn_qk(s)
                if late:
                    x_lo(2 * TILES + s - 3, 3)
                if s >= 1:
                    turn_probs(s - 1)
                if s >= 2:
                    context_norm(s - 2)
                turn_v(s)
            hidden(1, 0)
            x_lo(2 * TILES + 4, 3)
            softmax1(7)
            x_lo(2 * TILES + 5, 3)
            turn_probs(7)
            context_norm(6)
            hidden(1, 1)
            context_norm(7)
            hidden(1, 2)
            x_lo(2 * TILES + 6, 3)
            x_lo(2 * TILES + 7, 3)
            for k in range(3, len(GU1)):
                hidden(1, k)
            for t in range(TILES):
                add_residual(3 * TILES + t, bank[t])
                normalise(3 * TILES + t)


def kernel(L0_attn_x, L0_attn_Wqk_w, L0_attn_Wqk_b, L0_attn_Wv_w, L0_attn_Wv_b, L0_attn_Wo_w, L0_attn_Wo_b,
           L0_ffn_w1, L0_ffn_w1_scale, L0_ffn_w3, L0_ffn_w3_scale, L0_ffn_w2, L0_ffn_w2_scale,
           L1_attn_wq, L1_attn_bq, L1_attn_wk, L1_attn_bk, L1_attn_wv, L1_attn_bv, L1_attn_wl, L1_attn_bl,
           L1_ffn_gate_w, L1_ffn_up_w, L1_ffn_down_w, L1_ffn_gate_scale, L1_ffn_up_scale, L1_ffn_down_scale):
    import numpy as np
    from concourse import bacc
    from concourse.bass_utils import run_bass_kernel_spmd
    import ml_dtypes

    f = np.float32
    x = np.asarray(L0_attn_x).reshape(T, D)
    wqk, bqk = np.asarray(L0_attn_Wqk_w), np.asarray(L0_attn_Wqk_b)

    def chunked(w):
        return w.reshape(-1, P, w.shape[1]).transpose(1, 0, 2)

    def columns(w, chunks):
        w = np.asarray(w)
        full = np.zeros((chunks * P, w.shape[1]), f)
        full[:w.shape[0]] = w
        return full.reshape(chunks, P, KC, P).transpose(0, 3, 2, 1).reshape(chunks, P, 512)

    def rows(w, chunks):
        w = np.asarray(w)
        full = np.zeros((chunks * P, w.shape[0]), f)
        full[:w.shape[1]] = w.T
        return full.reshape(chunks, P, w.shape[0])

    def paired(a, b):
        return np.stack([a, b], 1).reshape(-1, P, 512)

    units = np.concatenate([
        paired(columns(L0_ffn_w1, J0), columns(L0_ffn_w3, J0)), rows(L0_ffn_w2, J0),
        rows(L1_attn_wq, KC), rows(L1_attn_wk, KC), rows(L1_attn_wv, KC),
        paired(columns(L1_ffn_gate_w, J1), columns(L1_ffn_up_w, J1)), rows(L1_ffn_down_w, J1)])
    unit_scale = np.concatenate([
        np.stack([np.asarray(L0_ffn_w1_scale), np.asarray(L0_ffn_w3_scale)], 1).reshape(2 * J0, KC),
        np.asarray(L0_ffn_w2_scale).T])
    wo = np.zeros((P, D), f)
    wo[:HD0] = np.asarray(L0_attn_Wo_w).T
    wo[HD0] = np.asarray(L0_attn_Wo_b)
    arrays = {
        "xT": x.reshape(B, N, KC, P).transpose(0, 3, 2, 1),
        "x": x,
        "wqkv": chunked(np.concatenate([wqk[0::2], wqk[1::2], np.asarray(L0_attn_Wv_w)]).T),
        "bqkv": np.concatenate([bqk[0::2], bqk[1::2], np.asarray(L0_attn_Wv_b)]),
        "wo": wo,
        "eye": np.eye(P, dtype=f),
        "eye16": np.eye(P, dtype=ml_dtypes.bfloat16),
        "units": units,
        "unit_scale": unit_scale,
        "b1": np.stack([np.asarray(L1_attn_bq), np.asarray(L1_attn_bk), np.asarray(L1_attn_bv)]),
        "ffn1_scale": np.stack([np.asarray(L1_ffn_gate_scale), np.asarray(L1_ffn_up_scale),
                                np.asarray(L1_ffn_down_scale)]),
    }
    arrays = {k: np.ascontiguousarray(v) for k, v in arrays.items()}
    nc = bacc.Bacc("TRN2", target_bir_lowering=False, num_devices=1, dynamic_dma_scratch_size=4096)
    aps = {k: nc.dram_tensor(k, v.shape, mybir.dt.from_np(v.dtype), kind="ExternalInput").ap()
           for k, v in arrays.items()}
    out = nc.dram_tensor("out", (T, D), F32, kind="ExternalOutput").ap()
    build(nc, out=out, **aps)
    got = run_bass_kernel_spmd(nc, [arrays], core_ids=[0])
    return got.results[0]["out"].reshape(B, N, D)
```

```python
from contextlib import ExitStack

import concourse.bass as bass
from concourse import mybir

P = 128
B, N, D = 2, 512, 512
T = B * N
TILES = T // P
TB = N // P
KC = D // P
H0, E0 = 8, 8
HD0 = H0 * E0
H1, E1 = 32, 16
J0 = 1792 // P
J1 = (1376 + P - 1) // P
EARLY = 4
LATE = 7
STACK_ON_VECTOR = 1
OT_ON_VECTOR = (2, 3, 4, 5)
EPS = 1e-5
PARTS = 3
ROWS = PARTS * PARTS * E0
STACK = 96
RAW = 2
SCAN = 4
SCANS = -(-3 * J1 // SCAN)
RING = 8
UNITS = 3 * J0 + 3 * KC + 3 * J1
U_DOWN0, U_QKV1, U_GU1, U_DOWN1 = 2 * J0, 3 * J0, 3 * J0 + 3 * KC, 3 * J0 + 3 * KC + 2 * J1

ALU = mybir.AluOpType
ACT = mybir.ActivationFunctionType
F32, F32R, BF16 = mybir.dt.float32, mybir.dt.float32r, mybir.dt.bfloat16
I32, U16 = mybir.dt.int32, mybir.dt.uint16
AX = mybir.AxisListType


def ring_index(u):
    return u if u < U_QKV1 else u - 3 * KC


def gate_up_order(chunks):
    early = [(j, b) for b in range(B) for j in range(EARLY)]
    return early + [(j, b) for j in range(EARLY, chunks) for b in range(B)]


GU0, GU1 = gate_up_order(J0), gate_up_order(J1)


def build(nc, xT, x, wqkv, bqkv, wo, eye, eye16, units, unit_scale, b1, ffn1_scale, out):
    with ExitStack() as ctx:
        def sb(name, shape, dt=F32, at=ctx):
            return at.enter_context(nc.sbuf_tensor(name, shape, dt))

        def sem(name):
            return ctx.enter_context(nc.semaphore(name))

        banks = [ctx.enter_context(nc.psum_tensor(f"banks{i}", [P, 2, 512], F32)) for i in range(4)]
        bank = [banks[i // 2][:, i % 2, :] for i in range(8)]

        x_tok = sb("x_tok", [P, TILES, D])
        xh = sb("xh", [P, KC, T], F32R)
        xl = sb("xl", [P, KC, T], F32R)
        ring = sb("ring", [P, RING, 2, 512], F32R)
        raw = sb("raw", [P, RAW, 512])
        ident = sb("ident", [P, P])
        ident16 = sb("ident16", [P, P], BF16)
        uscale = sb("uscale", [P, 3 * J0, KC])
        fscale = sb("fscale", [P, 3])
        z = sb("z", [P, 2, D])
        sg = sb("sg", [P, 2, N])
        hf = sb("hf", [P, 2, N])
        stats = sb("stats", [P, 2, 6])
        mv = sb("mv", [P, 2, 2])
        rstd = sb("rstd", [P, 2])
        half = sb("half", [P, 1])
        ones = sb("ones", [P, KC])
        low_bits = sb("low_bits", [P, 16])
        low_any = sb("low_any", [1, 1], I32)

        zeros = sb("zeros", [P, 512], BF16)

        s0 = ExitStack()
        QT = [None, None]
        KT = [None, None]
        Qst = [None, None]
        V0 = [None, None]
        QT[0] = sb("QT0", [P, H0, N], BF16, s0)
        KT[0] = sb("KT0", [P, H0, N], BF16, s0)
        Qst[0] = sb("Qst0", [P, TB, H0, STACK], BF16, s0)
        Kst = sb("Kst", [P, TB, H0, STACK], BF16, s0)
        V0[0] = sb("V00", [P, TB, H0, 32], F32, s0)
        QT[1] = sb("QT1", [P, H0, N], BF16, s0)
        KT[1] = sb("KT1", [P, H0, N], BF16, s0)
        Qst[1] = sb("Qst1", [P, TB, H0, STACK], BF16, s0)
        V0[1] = sb("V01", [P, TB, H0, 32], F32, s0)
        w_qkv = sb("w_qkv", [P, KC, 192], F32, s0)
        b_qkv = sb("b_qkv", [P, 192], F32, s0)
        w_o = sb("w_o", [P, D], F32, s0)
        qkv = sb("qkv", [P, TB, 192], F32, s0)
        smax = sb("smax", [P, TB, H0], F32, s0)
        srest = sb("srest", [P, TB, H0], F32, s0)
        OT = sb("OT", [P, 4, 256], F32, s0)
        o_rec = sb("o_rec", [P, 2, TB, 4], F32, s0)
        o_norm = sb("o_norm", [P, TB, P], F32, s0)
        oT = sb("oT", [P, N], F32, s0)
        with ExitStack() as s0x:
            xT0 = sb("xT0", [P, KC, T], F32, s0x)
            part = sb("part", [P, PARTS, 2, TB, HD0], BF16, s0x)
            rest = sb("rest", [P, 2, TB, HD0], F32, s0x)
        PT = [sb(f"PT{i}", [P, 4, TB, 256], F32, s0) for i in range(2)]
        s0.close()

        with ExitStack() as s1:
            hid0 = sb("hid0", [P, J0 - 2, 2, T], F32R, s1)
            with ExitStack() as s1x:
                scan = sb("scan", [P, 2, SCAN, 512], F32, s1x)
            hid0_last = sb("hid0_last", [P, 2, 2, T], F32R, s1)

        with ExitStack() as s2:
            w_qkv1 = sb("w_qkv1", [P, 3, KC, 2, D], F32R, s2)
            bias1 = sb("bias1", [P, 3, D], F32, s2)
            qpad = sb("qpad", [P, H1, 32], F32, s2)
            kpad = sb("kpad", [P, H1, 32], F32, s2)
            qT = sb("qT", [P, 32, H1], F32, s2)
            kT = sb("kT", [P, 32, H1], F32, s2)
            kbd = sb("kbd", [P, 32, 4, H1], F32, s2)
            vs = sb("vs", [P, E1, H1], F32, s2)
            vT = sb("vT", [P, 2, 32, E1], F32, s2)
            vbd = sb("vbd", [P, 32, 4, E1 + 1], F32, s2)
            mx1 = sb("mx1", [P, 32], F32, s2)
            pr = sb("pr", [P, 32, 32], F32, s2)
            prT = sb("prT", [P, 32, 32], F32, s2)
            rec1 = sb("rec1", [P, 32], F32, s2)
            cn = sb("cn", [P, E1, 32], F32, s2)
            ctx1 = sb("ctx1", [P, H1, E1], F32, s2)

        with ExitStack() as s3:
            hid1 = sb("hid1", [P, J1, 2, T], F32R, s3)

        got = {n: sem("got_" + n) for n in
               ("wqkv", "bqkv", "eye", "x", "wo", "uscale", "fscale", "bias1")}
        got_xT = [sem(f"got_xT{t}") for t in range(TB + 1)]
        raw_in = [sem(f"raw_in{i}") for i in range(RAW)]
        w_ready = sem("w_ready")
        pool_init = sem("pool_init")
        pool_zeros = sem("pool_zeros")
        dve_stack, act_stack = sem("dve_stack"), sem("act_stack")
        pool_v = sem("pool_v")
        pool_parts = sem("pool_parts")
        pool_pads = sem("pool_pads")
        pool_step = sem("pool_step")
        pool_rstd, pool_ve = sem("pool_rstd"), sem("pool_ve")
        pe_qkv0 = sem("pe_qkv0")
        pe_T = sem("pe_T")
        pe_S = sem("pe_S")
        pe_W = sem("pe_W")
        pe_ST = sem("pe_ST")
        pe_PV = sem("pe_PV")
        pe_OT = sem("pe_OT")
        pe_oT = sem("pe_oT")
        pe_y = sem("pe_y")
        pe_xT = sem("pe_xT")
        pe_G = sem("pe_G")
        pe_U = sem("pe_U")
        pe_down = sem("pe_down")
        pe_q1, pe_k1, pe_v1 = sem("pe_q1"), sem("pe_k1"), sem("pe_v1")
        pe_S1, pe_C1 = sem("pe_S1"), sem("pe_C1")
        act_T = sem("act_T")
        act_W, dve_W = sem("act_W"), sem("dve_W")
        act_exp = sem("act_exp")
        act_oT = sem("act_oT")
        act_xh = sem("act_xh")
        act_silu = sem("act_silu")
        act_hh = sem("act_hh")
        act_kbd, act_vbd, act_E1 = sem("act_kbd"), sem("act_vbd"), sem("act_E1")
        act_ve = sem("act_ve")
        dve_qkv0 = sem("dve_qkv0")
        dve_parts = sem("dve_parts")
        dve_T = sem("dve_T")
        dve_max = sem("dve_max")
        dve_mparts = sem("dve_mparts")
        dve_OT, act_OT = sem("dve_OT"), sem("act_OT")
        dve_on = sem("dve_on")
        dve_z, dve_var = sem("dve_z"), sem("dve_var")
        dve_xn = sem("dve_xn")
        dve_xl = sem("dve_xl")
        dve_h = sem("dve_h")
        dve_hl = sem("dve_hl")
        dve_qe, dve_ke = sem("dve_qe"), sem("dve_ke")
        dve_qT, dve_kT, dve_vT = sem("dve_qT"), sem("dve_kT"), sem("dve_vT")
        dve_sub, dve_prT, dve_cn = sem("dve_sub"), sem("dve_prT"), sem("dve_cn")
        dve_step = sem("dve_step")
        out_done = sem("out_done")
        scan_in = [sem(f"scan_in{i}") for i in range(2)]
        dve_scan, pe_low, dve_low = sem("dve_scan"), sem("pe_low"), sem("dve_low")

        def unit_used(r):
            layer = r >= U_QKV1
            k = r - layer * U_QKV1
            chunks, order, base = (J0, J1)[layer], (GU0, GU1)[layer], layer * len(GU0)
            if k < 2 * chunks:
                return (pe_G, pe_U)[k % 2], base + order.index((k // 2, B - 1)) + 1
            if k - 2 * chunks < chunks - LATE:
                return pe_down, layer * (J0 - LATE) + k - 2 * chunks + 1
            return pe_y, (2 + layer) * TILES

        def stack_read(n):
            if n == STACK_ON_VECTOR:
                return dve_T, 1
            return act_T, n + 1 - (n > STACK_ON_VECTOR)

        def output_read(u):
            if u in OT_ON_VECTOR:
                return dve_OT, OT_ON_VECTOR.index(u) + 1
            return act_OT, u + 1 - sum(v < u for v in OT_ON_VECTOR)

        def place(rows, a, qk):
            v = rows.rearrange("p t h (i j e) -> p (t h) i j e", i=PARTS, j=PARTS)
            return v[:, :, :, a, :] if qk else v[:, :, a, :, :]

        def spread(a, qk):
            src = part[:, a, qk].rearrange("p t (h e) -> p (t h) e", e=E0)
            return src.unsqueeze(2).to_broadcast([P, TB * H0, PARTS, E0])

        def bank0(t):
            return t % 2 if t < TB else t

        def hid(layer, j):
            if layer:
                return hid1[:, j]
            return hid0[:, j] if j < J0 - 2 else hid0_last[:, j - J0 + 2]

        def scan_units(i):
            return min(SCAN, 3 * J1 - i * SCAN)

        def gate_up_banks(layer, k):
            return (2, 3) if layer == 0 or k % 2 else (0, 1)

        def bank16(i):
            return bank[i].bitcast(BF16)

        block = ctx.enter_context(nc.Block())

        @block.sync
        def _(sp):
            for t in range(TB):
                cols = slice(t * P, (t + 1) * P)
                sp.dma_start(xT0[:, :, cols], xT[0][:, :, cols]).then_inc(got_xT[t], 16)
            sp.dma_start(b_qkv[:], bqkv.partition_broadcast(P)).then_inc(got["bqkv"], 16)
            sp.dma_start(xT0[:, :, N:], xT[1]).then_inc(got_xT[TB], 16)
            sp.dma_start(ident[:], eye).then_inc(got["eye"], 16)
            sp.dma_start(ident16[:], eye16).then_inc(got["eye"], 16)
            sp.dma_start(uscale[:], unit_scale.partition_broadcast(P)).then_inc(got["uscale"], 16)
            sp.dma_start(w_o[:], wo).then_inc(got["wo"], 16)
            sp.dma_start(x_tok[:], x.rearrange("(t p) d -> p t d", p=P)).then_inc(got["x"], 16)
            sp.dma_start(fscale[:], ffn1_scale.partition_broadcast(P)).then_inc(got["fscale"], 16)
            for u in range(UNITS):
                if u >= RAW:
                    sp.wait_ge(w_ready, u - RAW + 1)
                sp.dma_start(raw[:, u % RAW, :], units[u]).then_inc(raw_in[u % RAW], 16)
                if u == U_QKV1 + 3 * KC - 1:
                    sp.wait_ge(pe_y, 2 * TILES)
                    sp.dma_start(bias1[:], b1.partition_broadcast(P)).then_inc(got["bias1"], 16)
            for t in range(TILES):
                sp.wait_ge(dve_xn, 3 * TILES + t + 1)
                sp.dma_start(out[t * P:(t + 1) * P, :], x_tok[:, t, :]).then_inc(out_done, 16)
            sp.wait_ge(out_done, 16 * TILES)

        @block.gpsimd
        def _(pool):
            ms = nc.gpsimd.memset
            steps = [0]

            def step(ins):
                steps[0] += 1
                ins.then_inc(pool_step, 1)
                pool.wait_ge(pool_step, steps[0])

            def inverse_deviation(n):
                pool.wait_ge(dve_var, n + 1)
                if n >= 2:
                    pool.wait_ge(dve_xn, n - 1)
                nc.gpsimd.tensor_tensor(rstd[:, n % 2:n % 2 + 1], mv[:, n % 2, 1:2], half[:], ALU.pow)\
                    .then_inc(pool_rstd, 1)

            ms(zeros[:].bitcast(F32), 0.0).then_inc(pool_zeros, 1)
            ms(ones[:], 1.0)
            ms(half[:], -0.5)
            ms(Kst[:, :, :, ROWS:ROWS + 3], 1.0)
            ms(Kst[:, :, :, ROWS + 3:STACK], 0.0)
            for b in range(B):
                ms(Qst[b][:, :, :, ROWS:STACK], 0.0)
                ms(V0[b][:, :, :, E0:E0 + 1], 1.0)
                ms(V0[b][:, :, :, E0 + 1:], 0.0)
            ms(o_norm[:, :, HD0:HD0 + 1], 1.0)
            step(ms(o_norm[:, :, HD0 + 1:], 0.0))
            for a in (QT[0], KT[0], QT[1]):
                step(ms(a[STACK:P, :, :].bitcast(F32), 0.0))
            ms(KT[1][STACK:P, :, :].bitcast(F32), 0.0).then_inc(pool_init, 1)
            pool.wait_ge(pool_init, 1)
            for b in range(B):
                pool.wait_ge(dve_qkv0, TB * (b + 1))
                nc.gpsimd.tensor_copy(V0[b][:, :, :, 0:E0],
                                      qkv[:, :, 2 * HD0:].rearrange("p t (h e) -> p t h e", e=E0)).then_inc(pool_v, 1)

            pool.wait_ge(dve_stack, 1)
            pool.wait_ge(act_stack, 1)
            qk = qkv[:, :, 0:2 * HD0].rearrange("p t (q x) -> p q t x", q=2)
            step(nc.gpsimd.tensor_copy(part[:, 0], qk))
            step(nc.gpsimd.tensor_tensor(rest[:], qk, part[:, 0], ALU.subtract))
            step(nc.gpsimd.tensor_copy(part[:, 1], rest[:]))
            step(nc.gpsimd.tensor_tensor(rest[:], rest[:], part[:, 1], ALU.subtract))
            nc.gpsimd.tensor_copy(part[:, 2], rest[:]).then_inc(pool_parts, 1)

            pool.wait_ge(got["uscale"], 16)
            for u in range(UNITS):
                if u == RING:
                    for n in range(TILES):
                        inverse_deviation(n)
                if U_GU1 - TILES < u < U_GU1:
                    inverse_deviation(2 * TILES - 1 - U_GU1 + u)
                if u == U_GU1:
                    pool.wait_ge(pe_y, 2 * TILES)
                    ms(qpad[:, :, E1:], 0.0)
                    ms(kpad[:, :, E1:], 0.0).then_inc(pool_pads, 1)
                    inverse_deviation(2 * TILES - 1)
                    ms(kbd[:], 0.0)
                    ms(vbd[:, :, :, 0:E1], 0.0)
                    step(ms(vbd[:, :, :, E1:], 0.0))
                    for g in range(3):
                        step(ms(vbd[32 * g:32 * g + 32, :, g, E1:], 1.0))
                    ms(vbd[96:P, :, 3, E1:], 1.0).then_inc(pool_pads, 1)
                    pool.wait_ge(pool_pads, 2)
                    pool.wait_ge(got["bias1"], 16)
                if U_GU1 <= u < U_GU1 + TILES:
                    s = u - U_GU1
                    pool.wait_ge(act_ve, s + 1)
                    v = vs[:].rearrange("p e h -> p h e")
                    nc.gpsimd.tensor_tensor(v, v, bias1[:, 2, :].rearrange("p (h e) -> p h e", e=E1),
                                            ALU.add).then_inc(pool_ve, 1)
                    if s >= 2:
                        inverse_deviation(2 * TILES + s - 2)
                if u == U_GU1 + TILES:
                    for n in range(3 * TILES - 2, 3 * TILES):
                        inverse_deviation(n)
                w = raw[:, u % RAW, :]
                if U_QKV1 <= u < U_GU1:
                    k = u - U_QKV1
                    dst = w_qkv1[:, k // KC, k % KC]
                    if k % 2 == 0:
                        pool.wait_ge(pe_down, k // 2 + 1)
                else:
                    r = ring_index(u)
                    dst = ring[:, r % RING]
                    if r >= RING:
                        pool.wait_ge(*unit_used(r - RING))
                pool.wait_ge(raw_in[u % RAW], 16 * (u // RAW + 1))
                scale = uscale[:, u, :] if u < U_QKV1 else ones[:]
                by = scale.unsqueeze(2).to_broadcast([P, KC, P])
                w, hi, lo = (a.rearrange("p (c m) -> p c m", c=KC) for a in (w, dst[:, 0, :], dst[:, 1, :]))
                ins = nc.gpsimd.tensor_tensor(hi, w, by, ALU.mult)
                if u < U_QKV1:
                    ins = nc.gpsimd.tensor_tensor(w, w, by, ALU.mult)
                step(ins)
                nc.gpsimd.tensor_tensor(lo, w, hi.bitcast(F32), ALU.subtract).then_inc(w_ready, 1)
            for n in range(3 * TILES, 4 * TILES):
                inverse_deviation(n)

        @block.tensor
        def _(pe):
            def split_product(psum, sh, sl, mh, ml, first, last):
                nc.tensor.matmul(psum, sh, mh, start=first, stop=False)
                if ml is not None:
                    mm = nc.tensor.matmul(psum, sh, ml, start=False, stop=last and sl is None)
                if sl is not None:
                    mm = nc.tensor.matmul(psum, sl, mh, start=False, stop=last)
                return mm

            def project0(t):
                if t == 0:
                    pe.wait_ge(got["wqkv"], 16)
                if t <= TB:
                    pe.wait_ge(got_xT[t], 16)
                if t in (2, 3):
                    pe.wait_ge(dve_qkv0, t - 1)
                for c in range(KC):
                    mm = nc.tensor.matmul(bank[bank0(t)][:, 0:192], xT0[:, c, t * P:(t + 1) * P], w_qkv[:, c, :],
                                          start=(c == 0), stop=(c == KC - 1))
                mm.then_inc(pe_qkv0, 1)

            def transpose_stack(b, i, hh):
                n = 8 * b + i
                if n == 0 and hh == 0:
                    pe.wait_ge(got["eye"], 32)
                if i < 2 and hh == 0:
                    pe.wait_ge(dve_stack if n == 0 else act_stack, b + 1)
                if 2 <= n < 6 and hh == 0:
                    pe.wait_ge(dve_qkv0, n + 3)
                if n >= 6 and hh == 0:
                    pe.wait_ge(*stack_read(n - 6))
                src = (Kst, Qst[b])[i % 2]
                for t in range(TB):
                    c = hh * N + t * P
                    mm = nc.tensor.transpose(bank16(2 + n % 6)[0:STACK, c:c + P],
                                             src[:, t, 2 * (i // 2) + hh, :], ident16[:])
                if hh == 1:
                    mm.then_inc(pe_T, 1)

            def scores_for_max(b, tiles):
                for i in tiles:
                    h, t = divmod(i, TB)
                    n = b * H0 * TB + i
                    if n == 0:
                        pe.wait_ge(pool_init, 1)
                    if i % (2 * TB) == 0:
                        pe.wait_ge(*stack_read(8 * b + h))
                        pe.wait_ge(*stack_read(8 * b + h + 1))
                    if n >= 2:
                        pe.wait_ge(dve_max, n - 1)
                    nc.tensor.matmul(bank[n % 2], QT[b][:, h, t * P:(t + 1) * P], KT[b][:, h, :],
                                     start=True, stop=True).then_inc(pe_S, 1)

            def transpose_max(b, i):
                pe.wait_ge(dve_mparts, b + 1)
                if b == 0:
                    pe.wait_ge(*stack_read(11))
                if i >= 2:
                    pe.wait_ge((act_W, dve_W)[b], i - 1)
                for hh in range(2):
                    for t in range(TB):
                        c = hh * N + t * P
                        mm = nc.tensor.transpose(bank16((6, 0)[b] + i % 2)[64:STACK, c:c + P],
                                                 Qst[b][:, t, 2 * i + hh, 64:STACK], ident16[:])
                mm.then_inc(pe_W, 1)

            def scores_transposed(u, i):
                b, g, half = u // 4, u // 2 % 2, u % 2
                n = 4 * u + i
                if n % 2 == 0 and half == 0:
                    pe.wait_ge((act_W, dve_W)[b], (4 * g + i) // 2 + 1)
                if n >= 2:
                    pe.wait_ge(act_exp, n - 1)
                for kt in range(TB):
                    mm = nc.tensor.matmul(
                        banks[1 + n % 2][:, kt // 2, (kt % 2) * 256:(kt % 2) * 256 + 256],
                        KT[b][:, 4 * g + i, kt * P:(kt + 1) * P],
                        QT[b][:, 4 * g + i, half * 256:(half + 1) * 256], start=True, stop=True)
                mm.then_inc(pe_ST, 1)

            def weigh_values(u, kt):
                b, g = u // 4, u // 2 % 2
                if kt == 0:
                    pe.wait_ge(act_exp, 4 * u + 4)
                    pe.wait_ge(pool_v, b + 1)
                    if u >= 2:
                        pe.wait_ge(*output_read(u - 2))
                for i in range(4):
                    mm = nc.tensor.matmul(bank[6 + u % 2][32 * i:32 * i + 32, 0:256],
                                          V0[b][:, kt, 4 * g + i, :], PT[u % 2][:, i, kt, :],
                                          start=(kt == 0), stop=(kt == TB - 1), skip_group_check=True)
                if kt == TB - 1:
                    mm.then_inc(pe_PV, 1)

            def output_to_tokens(b):
                if b == 0:
                    pe.wait_ge(dve_W, 4)
                else:
                    pe.wait_ge(act_exp, 32)
                for u in range(4 * b, 4 * b + 4):
                    pe.wait_ge(*output_read(u))
                for g in range(2):
                    for t in range(TB):
                        mm = nc.tensor.transpose(bank[(0, 4)[b] + g][:, t * P:(t + 1) * P],
                                                 OT[:, 2 * g + t // 2, (t % 2) * P:(t % 2) * P + P], ident[:])
                    mm.then_inc(pe_OT, 1)

            def output_to_features(b):
                pe.wait_ge(dve_on, 2 * b + 2)
                pe.wait_ge(pool_init, 1)
                for t in range(TB):
                    mm = nc.tensor.transpose(bank[(0, 4)[b]][:, t * P:(t + 1) * P], o_norm[:, t, :], ident[:])
                mm.then_inc(pe_oT, 1)

            def output_product(t):
                if t % TB == 0:
                    pe.wait_ge(act_oT, t // TB + 1)
                if t == 0:
                    pe.wait_ge(got["wo"], 16)
                if t in (2, 3):
                    pe.wait_ge(dve_xl, t - 1)
                c = (t % TB) * P
                nc.tensor.matmul(bank[bank0(t)], oT[:, c:c + P], w_o[:], start=True, stop=True).then_inc(pe_y, 1)

            def transpose_x(layer, t, to):
                n = layer * TILES + t
                pe.wait_ge(dve_xn, n + 1)
                if layer == 2 and t > 0:
                    pe.wait_ge(*((dve_xl, n) if t < 5 else (dve_sub, TILES) if t < 7 else (dve_cn, TILES)))
                for c in range(KC):
                    mm = nc.tensor.transpose(bank[to][:, c * P:(c + 1) * P], x_tok[:, t, c * P:(c + 1) * P], ident[:])
                mm.then_inc(pe_xT, 1)

            def gate_up(layer, k, w_lo=True, between=lambda: None):
                j, b = (GU0, GU1)[layer][k]
                kk = k + layer * len(GU0)
                u = (0, U_GU1)[layer] + 2 * j
                if j == 0:
                    ready = (0, 2 * TILES)[layer] + TB * (b + 1)
                    pe.wait_ge(dve_xl, ready)
                if k == 0 and layer == 0:
                    pe.wait_ge(act_exp, 4 * 8)
                if k == 0 and layer == 1:
                    pe.wait_ge(dve_ke, TILES)
                if k == 1 and layer == 1:
                    pe.wait_ge(act_ve, TILES)
                    pe.wait_ge(dve_xl, 2 * TILES + 5)
                g, up = gate_up_banks(layer, k)
                for what, psum, done, free in ((0, bank[g], pe_G, act_silu), (1, bank[up], pe_U, dve_h)):
                    pe.wait_ge(w_ready, u + what + 1)
                    if layer == 0 and k >= 1:
                        pe.wait_ge(free, kk)
                    if layer == 1 and k >= 2:
                        pe.wait_ge(free, kk - 1)
                    w = ring[:, ring_index(u + what) % RING].rearrange("p s (c m) -> p s c m", c=KC)
                    cols = slice(b * N, (b + 1) * N)
                    for c in range(KC):
                        mm = split_product(psum, w[:, 0, c, :], w[:, 1, c, :] if w_lo else None, xh[:, c, cols], xl[:, c, cols],
                                           c == 0, c == KC - 1)
                    mm.then_inc(done, 1)
                    if what == 0:
                        between()

            def down_chunk(layer, j, t, w_lo):
                chunks = (J0, J1)[layer]
                h = hid(layer, j)
                w = ring[:, ring_index((U_DOWN0, U_DOWN1)[layer] + j) % RING]
                cols = slice(t * P, (t + 1) * P)
                return split_product(bank[t], h[:, 0, cols], h[:, 1, cols], w[:, 0, :],
                                     w[:, 1, :] if w_lo else None, j == 0, j == chunks - 1)

            def down(layer, between, w_lo=True):
                chunks = (J0, J1)[layer]
                base = layer * len(GU0)
                order = ([6, 7, 0, 1, 4, 5, 2, 3], [4, 5, 6, 7, 0, 1, 2, 3])[layer]
                for j in range(chunks - LATE):
                    pe.wait_ge(w_ready, (U_DOWN0, U_DOWN1)[layer] + j + 1)
                    pe.wait_ge(dve_hl, base + max(k for k, x in enumerate((GU0, GU1)[layer]) if x[0] == j) + 1)
                    for t in order:
                        if layer == 1 and j == 0 and t == 0:
                            pe.wait_ge(act_silu, base + 2 * chunks - 1)
                        if layer == 1 and j == 0 and t == 1:
                            pe.wait_ge(dve_h, base + 2 * chunks - 1)
                        if j == 0 and t == order[-2]:
                            pe.wait_ge(act_silu, base + 2 * chunks)
                        if j == 0 and t == order[-1]:
                            pe.wait_ge(dve_h, base + 2 * chunks)
                        mm = down_chunk(layer, j, t, w_lo)
                    mm.then_inc(pe_down, 1)
                pe.wait_ge(dve_hl, base + 2 * chunks)
                pe.wait_ge(w_ready, (U_DOWN0, U_DOWN1)[layer] + chunks)
                for t in range(TILES):
                    for j in range(chunks - LATE, chunks):
                        mm = down_chunk(layer, j, t, w_lo)
                    mm.then_inc(pe_y, 1)
                    between(t)

            def project1(t):
                cols = slice(t * P, (t + 1) * P)
                if t == 0:
                    pe.wait_ge(w_ready, U_GU1)
                pe.wait_ge(dve_xl, TILES + t + 1)
                if t == 0:
                    pe.wait_ge(dve_xl, TILES + 3)
                for i, (done, free) in enumerate(((pe_q1, dve_qe), (pe_k1, dve_ke), (pe_v1, act_ve))):
                    if t:
                        pe.wait_ge(free, t)
                    for c in range(KC):
                        sh, sl = xh[:, c, cols], xl[:, c, cols]
                        mm = split_product(bank[i], sh, sl, w_qkv1[:, i, c, 0, :], w_qkv1[:, i, c, 1, :],
                                           c == 0, c == KC - 1)
                    mm.then_inc(done, 1)

            def scores1(t):
                pe.wait_ge(dve_qT, t + 1)
                pe.wait_ge(act_kbd, t + 1)
                if t == 0:
                    pe.wait_ge(dve_xl, TILES + 6)
                if t:
                    pe.wait_ge(dve_sub, t)
                for s in range(8):
                    for j in range(4):
                        i = 4 * s + j
                        mm = nc.tensor.matmul(bank[4 + s // 4][32 * j:32 * j + 32, (s % 4) * P:(s % 4 + 1) * P],
                                              qT[:, i, :], kbd[:, i, :, :], start=True, stop=True,
                                              skip_group_check=True)
                mm.then_inc(pe_S1, 1)

            def context1(t):
                pe.wait_ge(dve_prT, t + 1)
                pe.wait_ge(act_vbd, t + 1)
                if t == 0:
                    pe.wait_ge(dve_xl, 2 * TILES)
                    pe.wait_ge(pool_pads, 2)
                if t:
                    pe.wait_ge(dve_cn, t)
                W = 4 * (E1 + 1)
                for s in range(8):
                    for g in range(4):
                        mm = nc.tensor.matmul(bank[6 + s // 4][32 * g:32 * g + 32, (s % 4) * W:(s % 4 + 1) * W],
                                              prT[:, 4 * s + g, :], vbd[:, 4 * s + g, :, :], start=True, stop=True,
                                              skip_group_check=True)
                mm.then_inc(pe_C1, 1)


            pe.wait_ge(pool_zeros, 1)
            for _ in range(10):
                nc.tensor.matmul(bank[2], zeros[:, 0:P], zeros[:], start=True, stop=True)
            for t in range(TILES):
                project0(t)
            for i in range(4):
                transpose_stack(0, i // 2, i % 2)
            for i in range(H0 * TB):
                scores_for_max(0, range(i, i + 1))
                if i < 6:
                    transpose_stack(0, i + 2, 0)
                    transpose_stack(0, i + 2, 1)
                if i >= 16:
                    transpose_stack(1, (i - 16) // 2, i % 2)
            scores_for_max(1, range(4))
            for i in range(4):
                transpose_max(0, i)
                scores_for_max(1, range(4 + 2 * i, 6 + 2 * i))
            for u in range(4):
                for i in range(4):
                    scores_transposed(u, i)
                    n = 12 + 2 * (4 * u + i)
                    scores_for_max(1, range(n, min(n + 2, 32)))
                    if u:
                        weigh_values(u - 1, i)
                    if u == 3:
                        transpose_max(1, i)
            for u in range(4, 8):
                for i in range(4):
                    scores_transposed(u, i)
                    weigh_values(u - 1, i)
                    if (u, i) == (5, 0):
                        output_to_tokens(0)
                    if (u, i) == (5, 2):
                        output_to_features(0)
                    if (u, i) == (5, 3):
                        output_product(0)
                        output_product(1)
                    if (u, i) == (7, 0):
                        transpose_x(0, 0, 0)
                        transpose_x(0, 1, 1)
                    if (u, i) == (7, 2):
                        output_product(2)
                        output_product(3)
            for kt in range(TB):
                weigh_values(7, kt)
            output_to_tokens(1)
            transpose_x(0, 2, 0)
            transpose_x(0, 3, 1)
            output_to_features(1)
            for t in range(TB, TILES):
                output_product(t)
            gate_up(0, 0)
            gate_up(0, 1)
            transpose_x(0, 4, 4)
            transpose_x(0, 5, 5)
            gate_up(0, 2)
            transpose_x(0, 6, 6)
            transpose_x(0, 7, 7)
            for k in range(3, len(GU0)):
                gate_up(0, k)
                if k == 2 * J0 - 4:
                    pe.wait_ge(dve_scan, SCANS + 1)
                    pe.wait_ge(dve_xl, 3)
                    nc.tensor.matmul(bank[0][0:KC, 0:1], ones[:], low_bits[:, 15:16], start=True, stop=True)\
                        .then_inc(pe_low, 1)

            pe.wait_ge(dve_low, 1)
            lo_parts = pe.value_load(low_any[0:1, 0:1])

            def after_down0(t):
                if t >= 3 and t % 2 == 1:
                    transpose_x(1, t - 3, t - 3)
                    transpose_x(1, t - 2, t - 2)

            down(0, after_down0)
            for s in range(TILES):
                project1(s)
                if s == 0:
                    transpose_x(1, 6, 6)
                    transpose_x(1, 7, 7)
                if s >= 1:
                    scores1(s - 1)
                if s >= 3:
                    transpose_x(2, s - 3, 3)
                if s >= 2:
                    context1(s - 2)
            def feed_forward1(w_lo):
                gate_up(1, 0, w_lo)
                gate_up(1, 1, w_lo, lambda: scores1(7))
                context1(6)
                gate_up(1, 2, w_lo)
                context1(7)
                transpose_x(2, 5, 4)
                gate_up(1, 3, w_lo)
                transpose_x(2, 6, 5)
                transpose_x(2, 7, 6)
                for k in range(4, len(GU1)):
                    gate_up(1, k, w_lo)
                down(1, lambda t: None, w_lo)

            with pe.If(lo_parts != 0):
                feed_forward1(True)
            with pe.If(lo_parts == 0):
                feed_forward1(False)

        @block.scalar
        def _(act):
            def stack_q(b):
                act.wait_ge(*((dve_parts, 1), (pool_parts, 1))[b])
                if b == 0:
                    act.wait_ge(pool_init, 1)
                for a in range(PARTS):
                    ins = nc.scalar.copy(place(Qst[b][:, :, :, 0:ROWS], a, 0), spread(a, 0))
                ins.then_inc(act_stack, 1)

            def stack_k1():
                act.wait_ge(pool_parts, 1)
                act.wait_ge(pe_T, 7)
                for a in range(PARTS):
                    nc.scalar.copy(place(Kst[:, :, :, 0:ROWS], a, 1), spread(a, 1))

            def evacuate_stack(n):
                act.wait_ge(pe_T, n + 1)
                b, i = divmod(n, 8)
                h = i // 2 * 2
                dst = (KT, QT)[i % 2][b][0:STACK, h:h + 2, :]
                nc.scalar.copy(dst, bank16(2 + n % 6)[0:STACK, :].rearrange("p (h n) -> p h n", h=2)).then_inc(act_T, 1)

            def evacuate_max0(i):
                act.wait_ge(pe_W, i + 1)
                nc.scalar.copy(QT[0][64:STACK, 2 * i:2 * i + 2, :],
                               bank16(6 + i % 2)[64:STACK, :].rearrange("p (h n) -> p h n", h=2))\
                    .then_inc(act_W, 1)

            def exponential(u, i):
                if u >= 2 and i == 0:
                    act.wait_ge(pe_PV, u - 1)
                n = 4 * u + i
                act.wait_ge(pe_ST, n + 1)
                nc.scalar.activation(PT[u % 2][:, i].rearrange("p k n -> p (k n)"),
                                     banks[1 + n % 2][:].rearrange("p k n -> p (k n)"), ACT.Exp).then_inc(act_exp, 1)

            def evacuate_output(u):
                act.wait_ge(pe_PV, u + 1)
                if u >= 4:
                    act.wait_ge(pe_OT, 2)
                nc.scalar.copy(OT[:, u % 4, :], bank[6 + u % 2][:, 0:256]).then_inc(act_OT, 1)

            def evacuate_oT(b):
                act.wait_ge(pe_oT, b + 1)
                nc.scalar.copy(oT[:], bank[(0, 4)[b]]).then_inc(act_oT, 1)

            def x_hi(n, bk):
                act.wait_ge(pe_xT, n + 1)
                t = n % TILES
                nc.scalar.copy(xh[:, :, t * P:(t + 1) * P],
                               bank[bk].rearrange("p (c n) -> p c n", c=KC)).then_inc(act_xh, 1)

            def silu(layer, k):
                kk = k + layer * len(GU0)
                act.wait_ge(pe_G, kk + 1)
                if kk >= 2:
                    act.wait_ge(dve_h, kk - 1)
                if layer and k == 0:
                    act.wait_ge(got["fscale"], 16)
                nc.scalar.activation(sg[:, kk % 2, :], bank[gate_up_banks(layer, k)[0]], ACT.Silu,
                                     scale=fscale[:, 0:1] if layer else 1.0).then_inc(act_silu, 1)

            def hidden_hi(layer, k):
                kk = k + layer * len(GU0)
                j, b = (GU0, GU1)[layer][k]
                act.wait_ge(dve_h, kk + 1)
                nc.scalar.copy(hid(layer, j)[:, 0, b * N:(b + 1) * N], hf[:, kk % 2, :]).then_inc(act_hh, 1)

            def hidden(layer, k):
                silu(layer, k)
                hidden_hi(layer, k)

            act.dma_start(w_qkv[:], wqkv).then_inc(got["wqkv"], 16)
            stack_q(0)
            for n in range(8):
                if n != STACK_ON_VECTOR:
                    evacuate_stack(n)
            stack_k1()
            stack_q(1)
            for n in range(8, 16):
                evacuate_stack(n)
            for i in range(4):
                evacuate_max0(i)
            for u in range(4):
                for i in range(4):
                    exponential(u, i)
                if 1 <= u < 3:
                    evacuate_output(u - 1)
            for u in range(4, 8):
                for i in range(4):
                    exponential(u, i)
                    if (u, i) == (5, 2):
                        evacuate_oT(0)
                    if (u, i) == (7, 0):
                        x_hi(0, 0)
                        x_hi(1, 1)
            evacuate_output(6)
            evacuate_output(7)
            x_hi(2, 0)
            x_hi(3, 1)
            evacuate_oT(1)
            hidden(0, 0)
            hidden(0, 1)
            x_hi(4, 4)
            x_hi(5, 5)
            hidden(0, 2)
            x_hi(6, 6)
            x_hi(7, 7)
            for k in range(3, len(GU0)):
                i = (k - 4) // 2
                if k % 2 == 0 and 0 <= i < SCANS:
                    if i == 0:
                        act.wait_ge(pe_y, TILES)
                    if i >= 2:
                        act.wait_ge(dve_scan, i - 1)
                    u = U_GU1 + i * SCAN
                    n = scan_units(i)
                    act.dma_start(scan[:, i % 2, 0:n, :], units[u:u + n].rearrange("u p m -> p u m"))\
                        .then_inc(scan_in[i % 2], 16)
                if k == 2 * (J0 - 2):
                    act.wait_ge(dve_scan, SCANS)
                hidden(0, k)
            for t in range(TILES):
                x_hi(TILES + t, t)

            def k_blocks(t):
                act.wait_ge(dve_kT, t + 1)
                if t == 0:
                    act.wait_ge(pool_pads, 2)
                else:
                    act.wait_ge(pe_S1, t)
                for g in range(4):
                    rows = slice(32 * g, 32 * g + 32)
                    ins = nc.scalar.copy(kbd[rows, :, g, :], kT[rows])
                ins.then_inc(act_kbd, 1)

            def v_blocks(t):
                act.wait_ge(dve_vT, t + 1)
                if t == 0:
                    act.wait_ge(pool_pads, 2)
                else:
                    act.wait_ge(pe_C1, t)
                for j in range(4):
                    to = vbd[32 * j:32 * j + 32].rearrange("p (s g) i e -> p s g i e", g=4)
                    for g in range(4):
                        ins = nc.scalar.copy(to[:, :, g, j, 0:E1],
                                             vT[32 * g:32 * g + 32, t % 2].rearrange("p (s i) e -> p s i e", i=4)[:, :, j, :])
                ins.then_inc(act_vbd, 1)

            def evacuate_v(t):
                act.wait_ge(pe_v1, t + 1)
                if t == 0:
                    act.wait_ge(pe_y, 2 * TILES)
                else:
                    act.wait_ge(dve_vT, t)
                nc.scalar.copy(vs[:].rearrange("p e h -> p h e"),
                               bank[2].rearrange("p (h e) -> p h e", e=E1)).then_inc(act_ve, 1)

            def exp1(t):
                act.wait_ge(dve_sub, t + 1)
                nc.scalar.activation(pr[:], pr[:], ACT.Exp, scale=E1 ** -0.5).then_inc(act_E1, 1)

            for s in range(TILES):
                evacuate_v(s)
                if s >= 3:
                    x_hi(2 * TILES + s - 3, 3)
                if s == 7:
                    k_blocks(s)
                if s >= 1:
                    exp1(s - 1)
                if s < 7:
                    k_blocks(s)
                if s >= 1:
                    v_blocks(s - 1)
            silu(1, 0)
            exp1(7)
            v_blocks(7)
            hidden_hi(1, 0)
            silu(1, 1)
            x_hi(2 * TILES + 5, 4)
            hidden_hi(1, 1)
            x_hi(2 * TILES + 6, 5)
            silu(1, 2)
            x_hi(2 * TILES + 7, 6)
            hidden_hi(1, 2)
            for k in range(3, len(GU1)):
                hidden(1, k)

        @block.vector
        def _(dve):
            tt, ts = nc.vector.tensor_tensor, nc.vector.tensor_scalar
            steps = [0]

            def step(ins):
                steps[0] += 1
                ins.then_inc(dve_step, 1)
                dve.wait_ge(dve_step, steps[0])

            def evacuate_qkv(t):
                if t == 0:
                    dve.wait_ge(got["bqkv"], 16)
                if t == TB:
                    dve.wait_ge(pool_v, 1)
                dve.wait_ge(pe_qkv0, t + 1)
                tt(qkv[:, t % TB, :], bank[bank0(t)][:, 0:192], b_qkv[:], ALU.add).then_inc(dve_qkv0, 1)

            def split_qk0():
                dve.wait_ge(dve_qkv0, TB)
                qk = qkv[:, :, 0:2 * HD0].rearrange("p t (q x) -> p q t x", q=2)
                step(nc.vector.tensor_copy(part[:, 0], qk))
                step(tt(rest[:], qk, part[:, 0], ALU.subtract))
                step(nc.vector.tensor_copy(part[:, 1], rest[:]))
                step(tt(rest[:], rest[:], part[:, 1], ALU.subtract))
                nc.vector.tensor_copy(part[:, 2], rest[:]).then_inc(dve_parts, 1)

            def stack_k0():
                dve.wait_ge(dve_parts, 1)
                dve.wait_ge(pool_init, 1)
                for a in range(PARTS):
                    ins = nc.vector.tensor_copy(place(Kst[:, :, :, 0:ROWS], a, 1), spread(a, 1))
                ins.then_inc(dve_stack, 1)

            def evacuate_stack0():
                dve.wait_ge(pe_T, STACK_ON_VECTOR + 1)
                nc.vector.tensor_copy(QT[0][0:STACK, 0:2, :],
                                      bank16(2 + STACK_ON_VECTOR)[0:STACK, :].rearrange("p (h n) -> p h n", h=2))\
                    .then_inc(dve_T, 1)

            def maxima(b, h):
                if b == 1 and h == 0:
                    dve.wait_ge(dve_mparts, 1)
                for t in range(TB):
                    n = (b * H0 + h) * TB + t
                    dve.wait_ge(pe_S, n + 1)
                    nc.vector.tensor_reduce(smax[:, t, h:h + 1], bank[n % 2], AX.X, ALU.max,
                                            negate=True).then_inc(dve_max, 1)

            def split_max(b):
                dve.wait_ge(dve_max, 32 * (b + 1))
                if b:
                    dve.wait_ge(dve_mparts, 1)
                if b == 0:
                    dve.wait_ge(pool_init, 1)
                to = [Qst[b][:, :, :, ROWS + a] for a in range(PARTS)]
                step(nc.vector.tensor_copy(to[0], smax[:]))
                step(tt(srest[:], smax[:], to[0], ALU.subtract))
                step(nc.vector.tensor_copy(to[1], srest[:]))
                step(tt(srest[:], srest[:], to[1], ALU.subtract))
                nc.vector.tensor_copy(to[2], srest[:]).then_inc(dve_mparts, 1)

            def evacuate_max1(i):
                dve.wait_ge(pe_W, 4 + i + 1)
                nc.vector.tensor_copy(QT[1][64:STACK, 2 * i:2 * i + 2, :],
                                      bank16(i % 2)[64:STACK, :].rearrange("p (h n) -> p h n", h=2))\
                    .then_inc(dve_W, 1)

            def evacuate_output(u):
                dve.wait_ge(pe_PV, u + 1)
                if u >= 4:
                    dve.wait_ge(pe_OT, 2)
                nc.vector.tensor_copy(OT[:, u % 4, :], bank[6 + u % 2][:, 0:256]).then_inc(dve_OT, 1)

            def normalise_output(b):
                if b == 0:
                    dve.wait_ge(pool_init, 1)
                else:
                    dve.wait_ge(dve_on, 2)
                    dve.wait_ge(pe_oT, 1)
                for g in range(2):
                    dve.wait_ge(pe_OT, 2 * b + g + 1)
                    o = bank[(0, 4)[b] + g].rearrange("p (t h e) -> p t h e", t=TB, h=4)
                    step(nc.vector.reciprocal(o_rec[:, g], o[:, :, :, E0]))
                    nc.vector.scalar_tensor_tensor(
                        out=o_norm[:, :, g * 32:(g + 1) * 32].rearrange("p t (h e) -> p t h e", h=4),
                        in0=o[:, :, :, 0:E0], scalar=HD0 ** -0.5,
                        in1=o_rec[:, g].unsqueeze(3).to_broadcast([P, TB, 4, E0]),
                        op0=ALU.mult, op1=ALU.mult).then_inc(dve_on, 1)

            def x_lo(n, bk):
                dve.wait_ge(act_xh, n + 1)
                t = n % TILES
                tt(xl[:, :, t * P:(t + 1) * P], bank[bk].rearrange("p (c n) -> p c n", c=KC),
                   xh[:, :, t * P:(t + 1) * P].bitcast(F32), ALU.subtract).then_inc(dve_xl, 1)

            def add_residual(n, src):
                layer, t = divmod(n, TILES)
                zz = z[:, n % 2, :]
                if layer != 2:
                    dve.wait_ge(pe_y, n + 1 - (TILES if layer == 3 else 0))
                if n == 0:
                    dve.wait_ge(got["x"], 16)
                elif n >= 2:
                    dve.wait_ge(dve_xn, n - 1)
                if layer == 3:
                    ins = nc.vector.scalar_tensor_tensor(out=zz, in0=src, scalar=fscale[:, 2:3], in1=x_tok[:, t, :],
                                                         op0=ALU.mult, op1=ALU.add)
                else:
                    ins = tt(zz, src, x_tok[:, t, :], ALU.add)
                ins.then_inc(dve_z, 1)
                dve.wait_ge(dve_z, n + 1)
                step(nc.vector.bn_stats(stats[:, n % 2, :], zz))
                if n >= 2:
                    dve.wait_ge(pool_rstd, n - 1)
                step(nc.vector.bn_aggr(mv[:, n % 2, :], stats[:, n % 2, :]))
                ts(mv[:, n % 2, 1:2], mv[:, n % 2, 1:2], EPS, None, ALU.add).then_inc(dve_var, 1)

            def normalise(n):
                dve.wait_ge(dve_var, n + 1)
                dve.wait_ge(pool_rstd, n + 1)
                ts(x_tok[:, n % TILES, :], z[:, n % 2, :], mv[:, n % 2, 0:1], rstd[:, n % 2:n % 2 + 1],
                   ALU.subtract, ALU.mult).then_inc(dve_xn, 1)

            def layernorm_pair(n, banks_):
                add_residual(n, bank[banks_[0]])
                add_residual(n + 1, bank[banks_[1]])
                normalise(n)
                normalise(n + 1)

            def hidden_product(layer, k):
                kk = k + layer * len(GU0)
                dve.wait_ge(act_silu, kk + 1)
                dve.wait_ge(pe_U, kk + 1)
                if kk >= 2:
                    dve.wait_ge(dve_hl, kk - 1)
                h = hf[:, kk % 2, :]
                if layer == 0:
                    tt(h, bank[3], sg[:, kk % 2, :], ALU.mult).then_inc(dve_h, 1)
                else:
                    if k == 0:
                        dve.wait_ge(got["fscale"], 16)
                    nc.vector.scalar_tensor_tensor(out=h, in0=bank[gate_up_banks(1, k)[1]], scalar=fscale[:, 1:2], in1=sg[:, kk % 2, :],
                                                   op0=ALU.mult, op1=ALU.mult).then_inc(dve_h, 1)

            def hidden_lo(layer, k):
                kk = k + layer * len(GU0)
                j, b = (GU0, GU1)[layer][k]
                dve.wait_ge(act_hh, kk + 1)
                h = hid(layer, j)
                tt(h[:, 1, b * N:(b + 1) * N], hf[:, kk % 2, :], h[:, 0, b * N:(b + 1) * N].bitcast(F32),
                   ALU.subtract).then_inc(dve_hl, 1)

            def hidden(layer, k):
                hidden_product(layer, k)
                hidden_lo(layer, k)

            for t in range(TB):
                evacuate_qkv(t)
            split_qk0()
            stack_k0()
            for t in range(TB, TILES):
                evacuate_qkv(t)
            evacuate_stack0()
            for h in range(H0):
                maxima(0, h)
            split_max(0)
            for h in range(H0):
                maxima(1, h)
            split_max(1)
            for i in range(4):
                evacuate_max1(i)
            evacuate_output(2)
            evacuate_output(3)
            normalise_output(0)
            layernorm_pair(0, (0, 1))
            evacuate_output(4)
            x_lo(0, 0)
            x_lo(1, 1)
            evacuate_output(5)
            layernorm_pair(2, (0, 1))
            normalise_output(1)
            x_lo(2, 0)
            x_lo(3, 1)
            layernorm_pair(4, (4, 5))
            hidden(0, 0)
            layernorm_pair(6, (6, 7))
            hidden(0, 1)
            x_lo(4, 4)
            x_lo(5, 5)
            hidden(0, 2)
            x_lo(6, 6)
            x_lo(7, 7)
            for k in range(3, len(GU0)):
                if k == 2 * (J0 - 2):
                    dve.wait_ge(dve_scan, SCANS + 1)
                if k == 2 * J0 - 2:
                    dve.wait_ge(pe_low, 1)
                    nc.vector.tensor_copy(low_any[:], bank[0][0:1, 0:1]).then_inc(dve_low, 1)
                hidden(0, k)
                i = (k - 6) // 2
                if k % 2 == 0 and 0 <= i < SCANS:
                    dve.wait_ge(scan_in[i % 2], 16 * (i // 2 + 1))
                    halves = scan[:, i % 2, 0:scan_units(i), :].rearrange("p u m -> p (u m)").bitcast(U16)
                    nc.vector.tensor_reduce(low_bits[:, i:i + 1], halves.rearrange("p (m w) -> p m w", w=2)[:, :, 0],
                                            AX.X, ALU.max).then_inc(dve_scan, 1)
                    if i == SCANS - 1:
                        dve.wait_ge(dve_scan, SCANS)
                        nc.vector.tensor_reduce(low_bits[:, 15:16], low_bits[:, 0:SCANS], AX.X, ALU.max)\
                            .then_inc(dve_scan, 1)
            for t in range(0, TILES, 2):
                layernorm_pair(TILES + t, (t, t + 1))
                if t >= 2:
                    x_lo(TILES + t - 2, t - 2)
                    x_lo(TILES + t - 1, t - 1)

            def evacuate1(t, i):
                if t == 0:
                    dve.wait_ge(got["bias1"], 16)
                    dve.wait_ge(pool_pads, 1)
                else:
                    dve.wait_ge((dve_qT, dve_kT)[i], t)
                dve.wait_ge((pe_q1, pe_k1)[i], t + 1)
                tt((qpad, kpad)[i][:, :, 0:E1], bank[i].rearrange("p (h e) -> p h e", e=E1),
                   bias1[:, i, :].rearrange("p (h e) -> p h e", e=E1), ALU.add).then_inc((dve_qe, dve_ke)[i], 1)

            def turn_qk(t):
                dve.wait_ge(dve_ke, t + 1)
                if t:
                    dve.wait_ge(pe_S1, t)
                nc.vector.transpose(qT[:].rearrange("p i h -> p h i"), qpad[:]).then_inc(dve_qT, 1)
                if t:
                    dve.wait_ge(act_kbd, t)
                nc.vector.transpose(kT[:].rearrange("p i h -> p h i"), kpad[:]).then_inc(dve_kT, 1)

            def turn_v(t):
                dve.wait_ge(pool_ve, t + 1)
                if t >= 2:
                    dve.wait_ge(act_vbd, t - 1)
                nc.vector.transpose(vT[:, t % 2].rearrange("p i e -> p e i"), vs[:]).then_inc(dve_vT, 1)

            def softmax1(t):
                dve.wait_ge(pe_S1, t + 1)
                if t:
                    dve.wait_ge(dve_sub, t)
                    dve.wait_ge(dve_prT, t)
                s = banks[2][:].rearrange("p b (i h) -> p (b i) h", h=H1)
                step(nc.vector.tensor_reduce(mx1[:], s, AX.X, ALU.max))
                tt(pr[:], s, mx1[:].unsqueeze(2).to_broadcast([P, 32, H1]), ALU.subtract).then_inc(dve_sub, 1)

            def turn_probs(t):
                dve.wait_ge(act_E1, t + 1)
                if t:
                    dve.wait_ge(pe_C1, t)
                nc.vector.transpose(prT[:], pr[:]).then_inc(dve_prT, 1)

            def context_divide(t):
                dve.wait_ge(pe_C1, t + 1)
                if t:
                    dve.wait_ge(dve_cn, t)
                c = banks[3][:, :, 0:16 * (E1 + 1)].rearrange("p b (i e) -> p b i e", e=E1 + 1)
                rec = rec1[:].rearrange("p (b i) -> p b i", b=2)
                step(nc.vector.reciprocal(rec, c[:, :, :, E1]))
                for i in range(2):
                    ins = tt(cn[:, :, 16 * i:16 * i + 16].rearrange("p e i -> p i e"), c[:, i, :, 0:E1],
                             rec1[:, 16 * i:16 * i + 16].unsqueeze(2).to_broadcast([P, 16, E1]), ALU.mult)
                ins.then_inc(dve_cn, 1)

            def context_residual(t):
                dve.wait_ge(dve_cn, t + 1)
                step(nc.vector.transpose(ctx1[:].rearrange("p h e -> p e h"), cn[:]))
                add_residual(2 * TILES + t, ctx1[:].rearrange("p h e -> p (h e)"))

            for s in range(TILES):
                evacuate1(s, 0)
                if s >= 3:
                    normalise(2 * TILES + s - 3)
                if s >= 1:
                    turn_v(s - 1)
                evacuate1(s, 1)
                if s == 0:
                    x_lo(TILES + 6, 6)
                    x_lo(TILES + 7, 7)
                if s == 7:
                    turn_qk(s)
                if s >= 1:
                    softmax1(s - 1)
                if s >= 3:
                    x_lo(2 * TILES + s - 3, 3)
                if s < 7:
                    turn_qk(s)
                if s >= 1:
                    turn_probs(s - 1)
                if s >= 2:
                    context_divide(s - 2)
                    if s < 7:
                        context_residual(s - 2)
            turn_v(7)
            softmax1(7)
            hidden_product(1, 0)
            context_residual(5)
            turn_probs(7)
            context_divide(6)
            normalise(2 * TILES + 5)
            context_residual(6)
            context_divide(7)
            hidden_product(1, 1)
            context_residual(7)
            normalise(2 * TILES + 6)
            normalise(2 * TILES + 7)
            x_lo(2 * TILES + 5, 4)
            x_lo(2 * TILES + 6, 5)
            x_lo(2 * TILES + 7, 6)
            hidden_lo(1, 0)
            hidden_lo(1, 1)
            hidden(1, 2)
            for k in range(3, len(GU1)):
                hidden(1, k)
            for t in range(TILES):
                add_residual(3 * TILES + t, bank[t])
                normalise(3 * TILES + t)


def kernel(L0_attn_x, L0_attn_Wqk_w, L0_attn_Wqk_b, L0_attn_Wv_w, L0_attn_Wv_b, L0_attn_Wo_w, L0_attn_Wo_b,
           L0_ffn_w1, L0_ffn_w1_scale, L0_ffn_w3, L0_ffn_w3_scale, L0_ffn_w2, L0_ffn_w2_scale,
           L1_attn_wq, L1_attn_bq, L1_attn_wk, L1_attn_bk, L1_attn_wv, L1_attn_bv, L1_attn_wl, L1_attn_bl,
           L1_ffn_gate_w, L1_ffn_up_w, L1_ffn_down_w, L1_ffn_gate_scale, L1_ffn_up_scale, L1_ffn_down_scale):
    import numpy as np
    from concourse import bacc
    from concourse.bass_utils import run_bass_kernel_spmd
    import ml_dtypes

    f = np.float32
    x = np.asarray(L0_attn_x).reshape(T, D)
    wqk, bqk = np.asarray(L0_attn_Wqk_w), np.asarray(L0_attn_Wqk_b)

    def chunked(w):
        return w.reshape(-1, P, w.shape[1]).transpose(1, 0, 2)

    def columns(w, chunks):
        w = np.asarray(w)
        full = np.zeros((chunks * P, w.shape[1]), f)
        full[:w.shape[0]] = w
        return full.reshape(chunks, P, KC, P).transpose(0, 3, 2, 1).reshape(chunks, P, 512)

    def rows(w, chunks):
        w = np.asarray(w)
        full = np.zeros((chunks * P, w.shape[0]), f)
        full[:w.shape[1]] = w.T
        return full.reshape(chunks, P, w.shape[0])

    def paired(a, b):
        return np.stack([a, b], 1).reshape(-1, P, 512)

    units = np.concatenate([
        paired(columns(L0_ffn_w1, J0), columns(L0_ffn_w3, J0)), rows(L0_ffn_w2, J0),
        rows(L1_attn_wq, KC), rows(L1_attn_wk, KC), rows(L1_attn_wv, KC),
        paired(columns(L1_ffn_gate_w, J1), columns(L1_ffn_up_w, J1)), rows(L1_ffn_down_w, J1)])
    unit_scale = np.concatenate([
        np.stack([np.asarray(L0_ffn_w1_scale), np.asarray(L0_ffn_w3_scale)], 1).reshape(2 * J0, KC),
        np.asarray(L0_ffn_w2_scale).T])
    wo = np.zeros((P, D), f)
    wo[:HD0] = np.asarray(L0_attn_Wo_w).T
    wo[HD0] = np.asarray(L0_attn_Wo_b)
    arrays = {
        "xT": x.reshape(B, N, KC, P).transpose(0, 3, 2, 1),
        "x": x,
        "wqkv": chunked(np.concatenate([wqk[0::2], wqk[1::2], np.asarray(L0_attn_Wv_w)]).T),
        "bqkv": np.concatenate([bqk[0::2], bqk[1::2], np.asarray(L0_attn_Wv_b)]),
        "wo": wo,
        "eye": np.eye(P, dtype=f),
        "eye16": np.eye(P, dtype=ml_dtypes.bfloat16),
        "units": units,
        "unit_scale": unit_scale,
        "b1": np.stack([np.asarray(L1_attn_bq), np.asarray(L1_attn_bk), np.asarray(L1_attn_bv)]),
        "ffn1_scale": np.stack([np.asarray(L1_ffn_gate_scale), np.asarray(L1_ffn_up_scale),
                                np.asarray(L1_ffn_down_scale)]),
    }
    arrays = {k: np.ascontiguousarray(v) for k, v in arrays.items()}
    nc = bacc.Bacc("TRN2", target_bir_lowering=False, num_devices=1, dynamic_dma_scratch_size=4096)
    aps = {k: nc.dram_tensor(k, v.shape, mybir.dt.from_np(v.dtype), kind="ExternalInput").ap()
           for k, v in arrays.items()}
    out = nc.dram_tensor("out", (T, D), F32, kind="ExternalOutput").ap()
    build(nc, out=out, **aps)
    got = run_bass_kernel_spmd(nc, [arrays], core_ids=[0])
    return got.results[0]["out"].reshape(B, N, D)
```
